# Optimizing a Trainium2 kernel written in Bass

```python
import numpy as np
import jax
import jax.numpy as jnp

def _softmax(x, axis=-1):
    return jax.nn.softmax(x, axis=axis)

def _gelu(x):
    return jax.nn.gelu(x, approximate=True)

def _silu(x):
    return jax.nn.silu(x)

def _sigmoid(x):
    return jax.nn.sigmoid(x)

def _layernorm(x, axis=-1, eps=1e-05):
    m = jnp.mean(x, axis=axis, keepdims=True)
    v = jnp.var(x, axis=axis, keepdims=True)
    return (x - m) / jnp.sqrt(v + eps)

def _scatter_add(tgt, idx, src, axis=0):
    return tgt.at[idx].add(src)

def _segment_sum(src, seg, n):
    return jax.ops.segment_sum(src, seg, n)
kernel_name = 'mk_adj_resnorm_d2_adj_r2_7e97f9'

def setup_inputs(seed: int=0):
    np.random.seed(seed)
    _w = jnp.asarray

    def _rec_inputs():
        import jax
        import jax.numpy as jnp
        _gk = jax.random.key(seed)
        x = -0.000929 + 1 * jax.random.normal(jax.random.fold_in(_gk, 1), (8192, 64), jnp.float32)
        _w = (1.0 + jnp.arange(8192, dtype=jnp.float32)) ** (-0.5)
        _w = _w / _w.mean()
        _pij = jnp.clip(0.000244141 * _w[:, None] * _w[None, :], 0.0, 1.0)
        _a = jax.random.uniform(jax.random.fold_in(_gk, 2), (8192, 8192)) < _pij
        _af = _a.astype(jnp.float32)
        adj = _af
        return (x, adj)
    x, adj = _rec_inputs()

    def _L0_gnn_setup():
        import jax, jax.numpy as jnp
        import numpy as np
        N, D_IN, D_OUT = (8192, 64, 64)
        AVG_DEG = 32.0
        L2_EPS = 1e-12
        key = jax.random.key(seed)
        kx, ka, kw, kb = jax.random.split(key, 4)
        X = jax.random.normal(kx, (N, D_IN), dtype=jnp.float32)
        adj = (jax.random.uniform(ka, (N, N)) < AVG_DEG / N).astype(jnp.float32)
        bound = 1.0 / np.sqrt(2 * D_IN)
        W = jax.random.uniform(kw, (2 * D_IN, D_OUT), dtype=jnp.float32, minval=-bound, maxval=bound)
        b = jax.random.uniform(kb, (D_OUT,), dtype=jnp.float32, minval=-bound, maxval=bound)
        return {'X': X, 'adj': adj, 'W': W, 'b': b}
    _L0_gnn_all = _L0_gnn_setup()
    _L0_gnn_in = {k: v for k, v in _L0_gnn_all.items() if k in ('W', 'b')}
    del _L0_gnn_all

    def _L1_gnn_setup():
        import jax, jax.numpy as jnp
        import numpy as np
        HOP = 2
        N = 8192
        HIDDEN = 64
        key = jax.random.key(seed)
        k1, k2, k3 = jax.random.split(key, 3)
        user_embs = jax.random.normal(k1, (N, HIDDEN), dtype=jnp.float32)
        adj = jax.random.uniform(k2, (N, N), dtype=jnp.float32)
        limit = float(np.sqrt(6.0 / (2 * HIDDEN + HIDDEN)))
        W = jax.random.uniform(k3, (HOP, 2 * HIDDEN, HIDDEN), dtype=jnp.float32, minval=-limit, maxval=limit)
        return {'user_embs': user_embs, 'adj': adj, 'W': W}
    _L1_gnn_all = _L1_gnn_setup()
    _L1_gnn_in = {k: v for k, v in _L1_gnn_all.items() if k in ('W',)}
    del _L1_gnn_all
    return {'x': x, 'adj': adj, 'L0_gnn_W': _L0_gnn_in['W'], 'L0_gnn_b': _L0_gnn_in['b'], 'L1_gnn_W': _L1_gnn_in['W']}

def reference(x, adj, L0_gnn_W, L0_gnn_b, L1_gnn_W):
    import jax
    import jax.numpy as jnp

    def _L0_gnn_ref(X, adj, W, b):
        import jax, jax.numpy as jnp
        import numpy as np
        N, D_IN, D_OUT = (8192, 64, 64)
        AVG_DEG = 32.0
        L2_EPS = 1e-12
        deg = jnp.clip(jnp.sum(adj, axis=1, keepdims=True) + 1.0, 1.0, None)
        h_neigh = (adj @ X + X) / deg
        concat = jnp.concatenate([X, h_neigh], axis=1)
        z = concat @ W + b
        out = jax.nn.relu(z)
        norm = jnp.linalg.norm(out, axis=1, keepdims=True)
        return out / jnp.maximum(norm, L2_EPS)

    def _L1_gnn_ref(user_embs, adj, W):
        import jax, jax.numpy as jnp
        import numpy as np
        HOP = 2
        N = 8192
        HIDDEN = 64
        x = user_embs
        for k in range(HOP):
            agg = adj @ x
            x = jnp.tanh(jnp.concatenate([agg, x], axis=1) @ W[k])
        return x
    x = _layernorm(x + _L0_gnn_ref(x, adj, L0_gnn_W, L0_gnn_b), axis=-1)
    x = _layernorm(x + _L1_gnn_ref(x, adj, L1_gnn_W), axis=-1)
    return x

_drawn_inputs = setup_inputs


def setup_inputs(seed=0):
    import zlib

    import numpy as np

    out = dict(_drawn_inputs(seed))
    spreads = {}
    factors = {}
    for name, (base, spread) in spreads.items():
        noise = np.random.default_rng([zlib.crc32(name.encode()), seed]).standard_normal(out[name].shape)
        drawn = base * np.exp(spread * noise) if base else spread * noise
        out[name] = jnp.asarray(drawn.astype(out[name].dtype))
    for name, factor in factors.items():
        out[name] = (out[name] * factor).astype(out[name].dtype)
    return out
```

```python
from contextlib import ExitStack

import concourse.bass as bass
from concourse import mybir

ALU = mybir.AluOpType
ACT = mybir.ActivationFunctionType
AX = mybir.AxisListType
F32 = mybir.dt.float32
BF16 = mybir.dt.bfloat16
F8 = mybir.dt.float8e4
U8 = mybir.dt.uint8
U32 = mybir.dt.uint32

P = 128
N = 8192
D = 64
BLK = 1024
NB = N // BLK
TB = BLK // P
HALF = BLK // 2
QH = TB // 2
NW = BLK // 16
STEPS = 2 * NB
ALL = STEPS * NB
TWO_A = NB * (NB + 1)

XHI, XMID, XLO, YLO, YHI, YMID, PARTS = 0, 64, 128, 192, 256, 320, 384
GROUPS = 3

ORDER_LOW = [7, 6, 5, 4, 3, 2, 1, 0]
ORDER_HIGH = [7, 0, 1, 2, 6, 5, 4, 3]

USES_1, USES_2A, USES_2B = 6, 4, 3
LN_EPS = 1e-5
L2_EPS = 1e-12


def gnn_kernel(nc, x, adj, w0, b0, w1, out):
    adj_t = adj.rearrange("(j q p) (i c) -> j i p q c", q=TB, p=P, c=BLK)
    x_t = x.rearrange("(j t p) d -> j p t d", t=TB, p=P)
    out_t = out.rearrange("(j t p) d -> j p t d", t=TB, p=P)

    with ExitStack() as ctx:
        def sb(name, shape, dt):
            return ctx.enter_context(nc.sbuf_tensor(name, shape, dt))

        def psum(name, shape, dt):
            return ctx.enter_context(nc.psum_tensor(name, shape, dt))

        def sem(name):
            return ctx.enter_context(nc.semaphore(name))

        packed = sb("packed", [P, NB * NB * 2 * TB * NW], U8)
        raw = sb("raw", [P, 4, 2 * BLK], F32)
        marks = sb("marks", [P, 2, QH, BLK], F8)
        planes = sb("planes", [P, 2, TB, HALF], F8)
        feats = sb("feats", [P, N // P, PARTS], BF16)
        zpart = sb("zpart", [P, NB, TB * D], F32)
        agg = [sb(f"agg{g}", [P, BLK], F32) for g in range(GROUPS)]
        featT = sb("featT", [D, BLK], F32)
        src = sb("src", [P, TB * D], F32)
        z = sb("z", [P, TB * D], F32)
        sq = agg[0][:, 0:TB * D]
        rest = agg[1][:, 0:TB * D]
        xin = agg[2][:, 0:TB * D]
        nonzero = sb("nonzero", [P, NB * TB, NB], F32)
        packsum = sb("packsum", [P, ALL], F32)
        pow2 = sb("pow2", [P, QH, NW], BF16)
        ident = sb("ident", [P, P], F32)
        bias = sb("bias", [P, D], F32)
        w_self = sb("w_self", [D, 3 * D], F32)
        w_a0 = sb("w_a0", [P, D], F32)
        w_a1 = sb("w_a1", [P, 2 * D], F32)
        w_y = sb("w_y", [P, D], F32)
        w_b1 = sb("w_b1", [P, 2 * D], F32)
        w_x2 = sb("w_x2", [P, D], F32)
        w_y_self = sb("w_y_self", [D, D], F32)
        w_x2_self = sb("w_x2_self", [D, D], F32)
        rdeg = sb("rdeg", [P, TB], F32)
        mean = sb("mean", [P, TB], F32)
        stat = sb("stat", [P, TB], F32)
        root = sb("root", [P, TB], F32)
        minus_half = sb("minus_half", [P, TB], F32)
        ones = sb("ones", [P, 1], F32)
        worth = sb("worth", [P, QH], F32)
        wrong = sb("wrong", [1, 1], F32)
        wrong_int = sb("wrong_int", [1, 1], mybir.dt.int32)

        general = packed[:, :].bitcast(F32)
        each = N // P * (D + 1)
        features = [general[:, n * each:(n + 1) * each].rearrange("p (t d) -> p t d", d=D + 1) for n in range(3)]

        acc = [psum(f"acc{g}", [P, 2, HALF], F32) for g in range(GROUPS)]
        ps_pack = psum("ps_pack", [P, HALF], F32)
        ps_epi = psum("ps_epi", [P, HALF], F32)

        consts = sem("consts")
        zeroed = sem("zeroed")
        weights_landed = sem("weights_landed")
        raw_landed = [sem(f"raw_landed{u}") for u in range(4)]
        marked = sem("marked")
        counted = sem("counted")
        pack_done = sem("pack_done")
        pack_saved = sem("pack_saved")
        planes_ready = sem("planes_ready")
        product_done = sem("product_done")
        acc_saved = sem("acc_saved")
        xin_landed = sem("xin_landed")
        split = sem("split")
        x_ready = sem("x_ready")
        x1_ready = sem("x1_ready")
        x2_ready = sem("x2_ready")
        src_landed = sem("src_landed")
        src_read = sem("src_read")
        epi_filled = sem("epi_filled")
        epi_drained = sem("epi_drained")
        chain = sem("chain")
        stat_ready = sem("stat_ready")
        root_ready = sem("root_ready")
        y_ready = sem("y_ready")
        z_ready = sem("z_ready")
        tanh_done = sem("tanh_done")
        out_ready = sem("out_ready")
        out_stored = sem("out_stored")
        sums_ready = sem("sums_ready")
        checked = sem("checked")
        x_landed = sem("x_landed")
        chunk_landed = [sem(f"chunk_landed{n}") for n in range(2)]
        turned_chunk = sem("turned_chunk")
        saved_chunk = sem("saved_chunk")
        added_chunk = sem("added_chunk")
        small_done = sem("small_done")
        steps = sem("steps")
        rooted = sem("rooted")
        tanned = sem("tanned")
        stored = sem("stored")
        passed = sem("passed")

        def pass_wait(eng):
            eng.sem_inc(passed, 1)

        def tiles(ap):
            return ap.rearrange("p (t d) -> p t d", d=D)

        def spread(ap):
            return ap.unsqueeze(2).to_broadcast([P, TB, D])

        def part(J, col):
            return feats[:, bass.ds(J * TB, TB), col:col + D]

        def bytes_of(J, I, h):
            width = TB * NW
            return packed[:, bass.ds(((J * NB + I) * 2 + h) * width, width)]

        def words_of(J, I, h):
            width = TB * NW
            ap = packed[:, bass.ds(((J * NB + I) * 2 + h) * width, width)].bitcast(U32)
            return ap.rearrange("p (a n) -> p a n", a=TB)

        def at_one(J):
            return J * STEPS

        def at_two(jj):
            return jj * (jj + 1) + ALL

        def at_three(J):
            return J * (J + 1) + (ALL + TWO_A)

        C1, C2A, C2B = 30, 8, 15
        EPI_2A = USES_1 * NB
        EPI_2B = EPI_2A + USES_2A * NB
        CH_2A = C1 * NB
        CH_2B = CH_2A + C2A * NB

        CONSTS = 6 + 2 * QH
        WEIGHTS = 16 * 15

        GC = [22, 5, 12]
        CHECK = 6
        NT = N // P
        CHUNKS = N // BLK
        g_base = [3, 3 + GC[0] * NT, 3 + (GC[0] + GC[1]) * NT]

        def unless_binary(eng):
            eng.wait_ge(checked, CHECK)
            return eng.value_load(wrong_int[:, :], min_val=0, max_val=1 << 24)

        block = ctx.enter_context(nc.Block())

        @block.sync
        def _(sp):
            def load_step(J, I, n, first):
                for u in range(4):
                    if not first:
                        sp.wait_ge(counted, 4 * n + (u - 3))
                        pass_wait(sp)
                    sp.dma_start(raw[:, u, :].rearrange("p (q c) -> p q c", q=2),
                                 adj_t[J, I, :, 2 * u:2 * u + 2, :]).then_inc(raw_landed[u], 16)

            def load_block(J, order, first=False):
                for k, I in enumerate(order):
                    load_step(J, I, J * NB + k, first and k == 0)
                    if k == 5:
                        if not first:
                            sp.wait_ge(src_read, J)
                        sp.dma_start(tiles(src[:, :]), x_t[J]).then_inc(src_landed, 16)

            load_block(0, ORDER_LOW, first=True)
            with sp.Fori(1, 4) as J:
                load_block(J, ORDER_LOW)
            with sp.Fori(4, NB) as J:
                load_block(J, ORDER_HIGH)
            with sp.Fori(0, NB) as J:
                sp.wait_ge(out_ready, J + 1)
                sp.dma_start(out_t[J], tiles(z[:, :])).then_inc(out_stored, 16)
            sp.wait_ge(out_stored, 16 * NB)

            with sp.If(unless_binary(sp) > 0):
                sp.wait_ge(product_done, ALL + TWO_A + NB * (NB + 1))
                sp.sem_inc(stored, 16)
                sp.dma_start(features[0][:, :, 0:D], x.rearrange("(t p) d -> p t d", p=P)).then_inc(x_landed, 16)
                for L in range(3):
                    with sp.Fori(0, NT) as J:
                        m = J + L * NT
                        for c in range(CHUNKS):
                            sp.wait_ge(turned_chunk, m * CHUNKS + (c + 1))
                            pass_wait(sp)
                            sp.dma_start(raw[:, c % 2, 0:BLK], adj[bass.ds(J * P, P), c * BLK:(c + 1) * BLK]
                                         ).then_inc(chunk_landed[c % 2], 16)
                        if L == 2:
                            sp.wait_ge(steps, J * GC[2] + (g_base[2] + GC[2]))
                            pass_wait(sp)
                            sp.dma_start(out[bass.ds(J * P, P), :], z[:, 0:D]).then_inc(stored, 16)
                sp.wait_ge(stored, 16 * (NT + 1))

        @block.scalar
        def _(act):
            act.wait_ge(zeroed, 3)
            for dst, src_ap in [
                (w_self[:, 0:D], w0[D:2 * D, :]), (w_self[:, 2 * D:3 * D], w0[0:D, :]),
                (w_a0[0:D, :], w0[D:2 * D, :]), (w_a0[D:P, :], w0[D:2 * D, :]),
                (w_a1[0:D, 0:D], w0[D:2 * D, :]), (w_a1[D:P, D:2 * D], w1[0, 0:D, :]),
                (w_y[0:D, :], w1[0, 0:D, :]), (w_y[D:P, :], w1[0, 0:D, :]),
                (w_b1[0:D, D:2 * D], w1[1, 0:D, :]), (w_b1[D:P, 0:D], w1[0, 0:D, :]),
                (w_x2[0:D, :], w1[1, 0:D, :]), (w_x2[D:P, :], w1[1, 0:D, :]),
                (w_y_self[:, :], w1[0, D:2 * D, :]), (w_x2_self[:, :], w1[1, D:2 * D, :]),
                (bias[:, :], b0.rearrange("(a d) -> a d", a=1).to_broadcast([P, D])),
            ]:
                act.dma_start(dst, src_ap).then_inc(weights_landed, 16)

            def count_block(J, order):
                for k, I in enumerate(order):
                    for u in range(4):
                        act.wait_ge(marked, J * 4 * NB + (4 * k + u + 1))
                        for q in range(2):
                            words = raw[:, u, q * BLK:(q + 1) * BLK]
                            ins = act.activation(words, words.bitcast(U32), ACT.Sign,
                                                 accum_out=nonzero[:, bass.ds(J * TB + (2 * u + q), 1), I])
                        ins.then_inc(counted, 1)

            with act.Fori(0, 4) as J:
                count_block(J, ORDER_LOW)
            with act.Fori(4, NB) as J:
                count_block(J, ORDER_HIGH)
            with act.Fori(0, 2 * NB) as n:
                act.wait_ge(z_ready, n + 1)
                act.activation(z[:, :], z[:, :], ACT.Tanh).then_inc(tanh_done, 1)

            with act.If(unless_binary(act) > 0):
                for L in (1, 2):
                    with act.Fori(0, NT) as J:
                        act.wait_ge(steps, J * GC[L] + (g_base[L] + 4))
                        act.activation(z[:, 0:D], z[:, 0:D], ACT.Tanh).then_inc(tanned, 1)

        @block.gpsimd
        def _(pool):
            pool.memset(w_self[:, :], 0.0).then_inc(zeroed, 1)
            pool.memset(w_a1[:, :], 0.0).then_inc(zeroed, 1)
            pool.memset(w_b1[:, :], 0.0).then_inc(zeroed, 1)
            pool.memset(pow2[:, :, :], 0.0).then_inc(consts, 1)
            pool.memset(ident[:, :], 0.0).then_inc(consts, 1)
            pool.memset(minus_half[:, :], -0.5).then_inc(consts, 1)
            pool.memset(feats[:, :, YLO:YLO + D], 0.0).then_inc(consts, 1)
            pool.memset(feats[:, :, YHI:YHI + 2 * D], 0.0).then_inc(consts, 1)
            pool.wait_ge(consts, 5)
            pool.affine_select(out=ident[:, :], in_=ident[:, :], compare_op=ALU.not_equal, fill=1.0,
                               base=0, pattern=[[-1, P]], channel_multiplier=1).then_inc(consts, 1)
            for q in range(QH):
                for half in range(2):
                    pool.wait_ge(consts, 6 + 2 * q + half)
                    pool.affine_select(out=pow2[:, q, :], in_=pow2[:, q, :], compare_op=ALU.not_equal,
                                       fill=float(2 ** (2 * q + half)) / 2, base=-half * NW,
                                       pattern=[[-1, NW]], channel_multiplier=1).then_inc(consts, 1)

            def split_feats(J, ap, col, lo, count, base, done):
                pool.tensor_copy(part(J, col), tiles(ap)).then_inc(split, 1)
                pool.wait_ge(split, count * 4 + (base + 1))
                pass_wait(pool)
                pool.tensor_tensor(tiles(rest), tiles(ap), part(J, col), ALU.subtract).then_inc(split, 1)
                pool.wait_ge(split, count * 4 + (base + 2))
                pool.tensor_copy(part(J, col + D), tiles(rest)).then_inc(split, 1)
                pool.wait_ge(split, count * 4 + (base + 3))
                pass_wait(pool)
                pool.tensor_tensor(part(J, lo), tiles(rest), part(J, col + D), ALU.subtract).then_inc(split, 1)
                pool.wait_ge(split, count * 4 + (base + 4))
                pool.sem_inc(done, 1)

            def power(n):
                pool.wait_ge(stat_ready, n)
                pool.tensor_tensor(root[:, :], stat[:, :], minus_half[:, :], ALU.pow).then_inc(root_ready, 1)

            for k, I in enumerate(ORDER_LOW):
                pool.dma_start(tiles(xin), x_t[I]).then_inc(xin_landed, 16)
                pool.wait_ge(xin_landed, 16 * (k + 1))
                split_feats(I, xin, XHI, XLO, k, 0, x_ready)

            def epilogue_one(J):
                power(J * 2 + 1)
                power(J * 2 + 2)
                pool.wait_ge(y_ready, J + 1)
                split_feats(J, z[:, :], YHI, YLO, J, 4 * NB, x1_ready)

            with pool.Fori(0, NB - 1) as J:
                epilogue_one(J)
            pool.wait_ge(product_done, ALL)
            pool.memset(feats[:, :, XHI:XLO + D], 0.0).then_inc(x2_ready, 1)
            epilogue_one(NB - 1)
            with pool.Fori(0, NB) as jj:
                pool.wait_ge(tanh_done, jj + 1)
                pass_wait(pool)
                split_feats(7 - jj, z[:, :], XHI, XLO, jj, 8 * NB, x2_ready)
            with pool.Fori(0, NB) as J:
                power(J + (2 * NB + 1))

            with pool.If(unless_binary(pool) > 0):
                def general_power(value):
                    pool.wait_ge(steps, value)
                    pool.tensor_tensor(root[:, 0:1], stat[:, 0:1], minus_half[:, 0:1], ALU.pow).then_inc(rooted, 1)

                with pool.Fori(0, NT) as J:
                    general_power(J * GC[0] + (g_base[0] + 12))
                    general_power(J * GC[0] + (g_base[0] + 20))
                with pool.Fori(0, NT) as J:
                    general_power(J * GC[2] + (g_base[2] + 11))

        @block.tensor
        def _(pe):
            def pack(J, s):
                h = s % 2
                pe.wait_ge(marked, J * (2 * STEPS) + (2 * s + 2))
                if not (isinstance(J, int) and s == 0):
                    pe.wait_ge(pack_saved, J * STEPS + s)
                pe.wait_ge(consts, CONSTS)
                pass_wait(pe)
                for a in range(TB):
                    for q in range(QH):
                        mm = pe.matmul(ps_pack[:, a * NW:(a + 1) * NW], marks[:, h, q, a * P:(a + 1) * P],
                                       pow2[:, q, :], start=q == 0, stop=q == QH - 1)
                mm.then_inc(pack_done, 1)

            def multiply(I, h, groups, start, stop):
                pass_wait(pe)
                for a in range(TB):
                    for g in groups:
                        mm = pe.matmul(acc[g][:, h, :], feats[:, I * TB + a, g * P:(g + 1) * P],
                                       planes[:, h, a, :], start=start and a == 0,
                                       stop=stop and a == TB - 1, skip_group_check=True)
                return mm

            def turn(use, half):
                pe.wait_ge(epi_drained, use)
                pe.wait_ge(consts, CONSTS)
                pass_wait(pe)
                for t in range(4):
                    tile = 4 * half + t
                    mm = pe.transpose(ps_epi[0:D, t * P:(t + 1) * P], src[:, tile * D:(tile + 1) * D],
                                      ident[:, :])
                mm.then_inc(epi_filled, 1)

            def weigh(use, first_tile, count, products, width):
                pe.wait_ge(epi_drained, use)
                pe.wait_ge(weights_landed, WEIGHTS)
                pass_wait(pe)
                for t in range(count):
                    rows = slice((first_tile + t) * P, (first_tile + t + 1) * P)
                    for n, (lhs, w, col) in enumerate(products):
                        at = t * width + col
                        mm = pe.matmul(ps_epi[:, at:at + w.shape[1]], lhs[:, rows], w, start=n == 0,
                                       stop=n == len(products) - 1, skip_group_check=True)
                mm.then_inc(epi_filled, 1)

            own = featT[:, :]
            ONE = [(own, w_self[:, :], 0), (agg[0], w_a0[:, :], 0), (agg[1], w_a1[:, :], 0), (agg[2], w_y[:, :], D)]
            TWO = [(agg[1], w_b1[:, :], 0), (agg[2], w_y[:, :], 0), (own, w_y_self[:, :], 0), (agg[0], w_x2[:, :], D)]
            THREE = [(agg[0], w_x2[:, :], 0), (agg[1][0:D, :], w_x2[0:D, :], 0), (own, w_x2_self[:, :], 0)]

            def epilogue_one(J, piece):
                base = J * USES_1
                if piece == 0:
                    pe.wait_ge(src_landed, J * 16 + 16)
                    turn(base, 0)
                elif piece == 1:
                    turn(base + 1, 1)
                elif piece == 2:
                    pe.wait_ge(acc_saved, J * 2 + 2)
                    weigh(base + 2, 0, 2, ONE, 3 * D)
                    weigh(base + 3, 2, 2, ONE, 3 * D)
                else:
                    weigh(base + 4, 4, 2, ONE, 3 * D)
                    weigh(base + 5, 6, 2, ONE, 3 * D)

            def block_one(J, order, first=False, last=False):
                for s in range(STEPS):
                    k, h = divmod(s, 2)
                    I = order[k]
                    if not (last and s == STEPS - 1):
                        pack(J, s + 1)
                    pe.wait_ge(planes_ready, J * STEPS + (s + 1))
                    if k == 0 and not first:
                        pe.wait_ge(acc_saved, J * 2 + (h - 1))
                    pe.wait_ge(x_ready, k + 1 if first else NB)
                    ends = k in (0, NB - 1)
                    if not (first or ends):
                        with pe.If(J > I):
                            pe.wait_ge(x1_ready, I + 1)
                            multiply(I, h, [2], False, False)
                    if k == NB - 1 and not first:
                        pe.wait_ge(x1_ready, I + 1)
                    multiply(I, h, range(3) if ends else range(2), k == 0, k == NB - 1).then_inc(product_done, 1)
                    if not first and s < 4:
                        epilogue_one(J - 1, s)

            pack(0, 0)
            block_one(0, ORDER_LOW, first=True)
            with pe.Fori(1, 4) as J:
                block_one(J, ORDER_LOW)
            with pe.Fori(4, NB - 1) as J:
                block_one(J, ORDER_HIGH)
            block_one(NB - 1, ORDER_HIGH, last=True)
            for piece in range(4):
                epilogue_one(NB - 1, piece)

            pe.wait_ge(pack_saved, ALL)
            pe.wait_ge(counted, 2 * ALL)
            pe.wait_ge(checked, 3)
            pe.matmul(ps_pack[0:1, 0:ALL], ones[:, :], packsum[:, :], start=True, stop=False)
            counts = nonzero[:, :, :].rearrange("p (j h q) i -> p q j i h", j=NB, h=2)
            for q in range(QH):
                mm = pe.matmul(ps_pack[0:1, 0:ALL], worth[:, q:q + 1], counts[:, q], start=False, stop=q == QH - 1)
            mm.then_inc(sums_ready, 1)

            with pe.Fori(0, NB) as jj:
                J = 7 - jj
                for I in range(NB - 1, -1, -1):
                    with pe.If(J <= I):
                        for h in range(2):
                            pe.wait_ge(planes_ready, at_two(jj) + (2 * (7 - I) + h + 1))
                            if I == NB - 1:
                                pe.wait_ge(acc_saved, jj * 2 + (2 * NB - 1 + h))
                                pass_wait(pe)
                            pe.wait_ge(x1_ready, NB)
                            if h == 0:
                                with pe.If(J < I):
                                    pe.wait_ge(x2_ready, 9 - I)
                                pe.wait_ge(x2_ready, 1)
                            multiply(I, h, range(3), I == NB - 1, False).then_inc(product_done, 1)
                base = jj * USES_2A + EPI_2A
                pe.wait_ge(chain, jj * C2A + (CH_2A + 2))
                turn(base, 0)
                turn(base + 1, 1)
                pe.wait_ge(acc_saved, jj * 2 + (2 * NB + 2))
                pass_wait(pe)
                weigh(base + 2, 0, 4, TWO, 2 * D)
                weigh(base + 3, 4, 4, TWO, 2 * D)

            with pe.Fori(0, NB) as J:
                for I in range(NB):
                    with pe.If(J >= I):
                        for h in range(2):
                            pe.wait_ge(planes_ready, at_three(J) + (2 * I + h + 1))
                            if I == 0:
                                pe.wait_ge(acc_saved, J * 2 + (4 * NB - 1 + h))
                            pe.wait_ge(x2_ready, NB + 1)
                            multiply(I, h, range(2), I == 0, False).then_inc(product_done, 1)
                base = J * USES_2B + EPI_2B
                pe.wait_ge(chain, J * C2B + (CH_2B + 2))
                turn(base, 0)
                turn(base + 1, 1)
                pe.wait_ge(acc_saved, J * 2 + (4 * NB + 2))
                pass_wait(pe)
                weigh(base + 2, 0, 8, THREE, D)

            with pe.If(unless_binary(pe) > 0):
                pe.sem_inc(turned_chunk, 2)
                pe.sem_inc(added_chunk, 1)
                pe.wait_ge(x_landed, 16)
                for L in range(3):
                    with pe.Fori(0, NT) as J:
                        m = J + L * NT
                        for c in range(CHUNKS):
                            pe.wait_ge(chunk_landed[c % 2], m * (16 * CHUNKS // 2) + 16 * (c // 2 + 1))
                            pass_wait(pe)
                            if L == 0 and c == 0:
                                pe.wait_ge(steps, 3)
                            pe.wait_ge(saved_chunk, m * CHUNKS + (c + 1))
                            pass_wait(pe)
                            for a in range(TB):
                                mm = pe.transpose(acc[0][:, a // 4, (a % 4) * P:(a % 4 + 1) * P],
                                                  raw[:, c % 2, a * P:(a + 1) * P], ident[:, :])
                            mm.then_inc(turned_chunk, 1)
                            pe.wait_ge(saved_chunk, m * CHUNKS + (c + 2))
                            pass_wait(pe)
                            for a in range(TB):
                                mm = pe.matmul(ps_epi[:, 0:D + 1], agg[0][:, a * P:(a + 1) * P],
                                               features[L][:, c * TB + a, :], start=c + a == 0,
                                               stop=c == CHUNKS - 1 and a == TB - 1)
                            mm.then_inc(added_chunk, 1)
                        at = J * GC[L] + g_base[L]
                        pe.wait_ge(steps, at + 2)
                        pass_wait(pe)
                        pe.transpose(ps_pack[0:D, 0:P], z[:, 0:D], ident[:, :])
                        pe.transpose(ps_pack[0:D, P:2 * P], src[:, 0:D], ident[:, :]).then_inc(small_done, 1)
                        pe.wait_ge(steps, at + 3)
                        pass_wait(pe)
                        if L == 0:
                            pe.matmul(acc[1][:, 0, 0:3 * D], featT[:, P:2 * P], w_self[:, :], start=True, stop=True)
                            pe.matmul(acc[1][:, 0, 0:D], featT[:, 0:P], w_a0[0:D, :], start=False, stop=True,
                                      skip_group_check=True).then_inc(small_done, 1)
                        else:
                            w, w_own = (w_y, w_y_self) if L == 1 else (w_x2, w_x2_self)
                            pe.matmul(acc[1][:, 0, 0:D], featT[:, P:2 * P], w_own[:, :], start=True, stop=False)
                            pe.matmul(acc[1][:, 0, 0:D], featT[:, 0:P], w[0:D, :], start=False,
                                      stop=True).then_inc(small_done, 1)

        @block.vector
        def _(dve):
            def mark(J, s, first=False):
                k, h = divmod(s, 2)
                for u in (2 * h, 2 * h + 1):
                    dve.wait_ge(raw_landed[u], J * (16 * NB) + 16 * (k + 1))
                    if not first:
                        dve.wait_ge(pack_done, J * STEPS + (s - 1))
                    out_ap = marks[:, h, 2 * (u % 2):2 * (u % 2) + 2, :].rearrange("p q c -> p (q c)")
                    dve.tensor_scalar(out_ap.bitcast(U8), raw[:, u, :], 1.0, 64.0, ALU.is_equal,
                                      ALU.mult).then_inc(marked, 1)

            def save_pack(J, s, I):
                dve.wait_ge(pack_done, J * STEPS + (s + 1))
                dve.tensor_scalar(bytes_of(J, I, s % 2), ps_pack[:, :], 1.0, None, ALU.mult, ALU.add,
                                  accum_out=packsum[:, bass.ds((J * NB + I) * 2 + s % 2, 1)]).then_inc(pack_saved, 1)

            def expand(J, I, h, n, first=False):
                if not first:
                    dve.wait_ge(product_done, n - 1)
                    pass_wait(dve)
                words = words_of(J, I, h)
                wide = planes[:, h, :, :].bitcast(U32)
                for bit in range(8):
                    shift, op = (6 - bit, ALU.logical_shift_left) if bit < 7 else (1, ALU.logical_shift_right)
                    ins = dve.tensor_scalar(wide[:, :, bit * NW // 4:(bit + 1) * NW // 4], words, shift,
                                            0x40404040, op, ALU.bitwise_and)
                ins.then_inc(planes_ready, 1)

            def save_acc(h, done, groups, scratch_free):
                scratch_free()
                dve.wait_ge(product_done, done)
                pass_wait(dve)
                for g in groups:
                    ins = dve.tensor_scalar(agg[g][:, h * HALF:(h + 1) * HALF], acc[g][:, h, :], 0.5, None, ALU.mult)
                ins.then_inc(acc_saved, 1)

            class Chain:
                def __init__(self, base, count=0):
                    self.base, self.count = base, count

                def wait(self):
                    dve.wait_ge(chain, self.base + self.count)
                    pass_wait(dve)

                def step(self, ins):
                    ins.then_inc(chain, 1)
                    self.count += 1

            def turned(c, use, half):
                dve.wait_ge(epi_filled, use + 1)
                c.step(dve.tensor_copy(featT[:, half * HALF:(half + 1) * HALF], ps_epi[0:D, :]))
                c.wait()
                dve.sem_inc(epi_drained, 1)

            def layernorm(c, powers):
                c.wait()
                c.step(dve.tensor_reduce(mean[:, :], tiles(z[:, :]), AX.X, ALU.add))
                c.wait()
                c.step(dve.tensor_scalar(mean[:, :], mean[:, :], -1.0 / D, None, ALU.mult))
                c.wait()
                c.step(dve.tensor_tensor(tiles(z[:, :]), tiles(z[:, :]), spread(mean[:, :]), ALU.add))

            def variance(c):
                c.wait()
                c.step(dve.tensor_tensor(sq, z[:, :], z[:, :], ALU.mult))
                c.wait()
                c.step(dve.tensor_reduce(stat[:, :], tiles(sq), AX.X, ALU.add))
                c.wait()
                c.step(dve.tensor_scalar(stat[:, :], stat[:, :], 1.0 / D, LN_EPS, ALU.mult, ALU.add))
                c.wait()
                dve.sem_inc(stat_ready, 1)

            def scale(c, root_count):
                dve.wait_ge(root_ready, root_count)
                c.step(dve.tensor_tensor(tiles(z[:, :]), tiles(z[:, :]), spread(root[:, :]), ALU.mult))
                c.wait()

            def epilogue_one(J, piece):
                base = J * USES_1
                if piece == 0:
                    c = Chain(J * C1, 0)
                    dve.wait_ge(counted, J * (4 * NB) + 4 * NB)
                    c.step(dve.tensor_reduce(rdeg[:, :], nonzero[:, bass.ds(J * TB, TB), :], AX.X, ALU.add))
                    c.wait()
                    c.step(dve.tensor_scalar(rdeg[:, :], rdeg[:, :], 1.0, 1.0, ALU.add, ALU.max))
                    c.wait()
                    c.step(dve.reciprocal(rdeg[:, :], rdeg[:, :]))
                    turned(c, base, 0)
                elif piece == 1:
                    turned(Chain(J * C1, 4), base + 1, 1)
                elif piece in (2, 3):
                    c = Chain(J * C1, 5 if piece == 2 else 11)
                    for n in (0, 1):
                        pair = 2 * (piece - 2) + n
                        dve.wait_ge(epi_filled, base + (3 + pair))
                        cols = slice(2 * pair * D, (2 * pair + 2) * D)
                        ps = ps_epi[:, 0:6 * D].rearrange("p (t c) -> p t c", t=2)
                        c.step(dve.tensor_copy(tiles(zpart[:, J, cols]), ps[:, :, D:2 * D]))
                        c.step(dve.tensor_tensor(tiles(z[:, cols]), ps[:, :, 0:D],
                                                 rdeg[:, 2 * pair:2 * pair + 2].unsqueeze(2).to_broadcast([P, 2, D]),
                                                 ALU.mult))
                        c.wait()
                        c.step(dve.tensor_tensor(tiles(z[:, cols]), tiles(z[:, cols]), ps[:, :, 2 * D:3 * D], ALU.add))
                        c.wait()
                        dve.sem_inc(epi_drained, 1)
                elif piece == 4:
                    c = Chain(J * C1, 17)
                    c.step(dve.tensor_tensor(tiles(z[:, :]), tiles(z[:, :]),
                                             bias[:, :].unsqueeze(1).to_broadcast([P, TB, D]), ALU.add))
                    c.wait()
                    c.step(dve.scalar_tensor_tensor(sq, z[:, :], 0.0, z[:, :], ALU.max, ALU.mult))
                    c.wait()
                    c.step(dve.tensor_reduce(stat[:, :], tiles(sq), AX.X, ALU.add))
                    c.wait()
                    c.step(dve.tensor_scalar(stat[:, :], stat[:, :], L2_EPS ** 2, None, ALU.max))
                    c.wait()
                    dve.sem_inc(stat_ready, 1)
                elif piece == 5:
                    c = Chain(J * C1, 21)
                    dve.wait_ge(root_ready, J * 2 + 1)
                    c.step(dve.scalar_tensor_tensor(tiles(z[:, :]), tiles(z[:, :]), 0.0, spread(root[:, :]),
                                                    ALU.max, ALU.mult))
                    c.wait()
                    c.step(dve.tensor_tensor(z[:, :], z[:, :], src[:, :], ALU.add))
                    c.wait()
                    dve.sem_inc(src_read, 1)
                    layernorm(c, None)
                elif piece == 6:
                    variance(Chain(J * C1, 26))
                else:
                    c = Chain(J * C1, 29)
                    scale(c, J * 2 + 2)
                    dve.sem_inc(y_ready, 1)

            def block_one(J, order, first=False, last=False):
                for s in range(STEPS):
                    k, h = divmod(s, 2)
                    nxt = (order + [7])[(s + 1) // 2]
                    if not (last and s + 1 >= STEPS):
                        save_pack(J, s + 1, nxt) if s + 1 < STEPS else save_pack(J + 1, 0, nxt)
                        dve.wait_ge(pack_saved, J * STEPS + (s + 2))
                        over = s + 1 >= STEPS
                        expand(J + 1 if over else J, nxt, (s + 1) % 2, J * STEPS + (s + 1), first and s == 0)
                    if not (last and s + 2 >= STEPS):
                        mark(J, s + 2)
                    if not first:
                        if s < 8:
                            epilogue_one(J - 1, s)
                    if k == NB - 1:
                        save_acc(h, J * STEPS + (s + 1), range(3),
                                 lambda: dve.wait_ge(x_ready, NB) if first else dve.wait_ge(x1_ready, J))

            dve.memset(ones[:, :], 1.0).then_inc(checked, 1)
            dve.wait_ge(consts, CONSTS)
            dve.tensor_reduce(worth[:, :], pow2[:, :, :], AX.X, ALU.add).then_inc(checked, 1)
            dve.wait_ge(checked, 2)
            dve.tensor_scalar(worth[:, :], worth[:, :], -2.0, None, ALU.mult).then_inc(checked, 1)
            mark(0, 0, first=True)
            mark(0, 1, first=True)
            save_pack(0, 0, 7)
            dve.wait_ge(pack_saved, 1)
            expand(0, 7, 0, 0, first=True)
            block_one(0, ORDER_LOW, first=True)
            with dve.Fori(1, 4) as J:
                block_one(J, ORDER_LOW)
            with dve.Fori(4, NB - 1) as J:
                block_one(J, ORDER_HIGH)
            block_one(NB - 1, ORDER_HIGH, last=True)
            for piece in range(8):
                epilogue_one(NB - 1, piece)

            def own_features(c, hi, mid, lo):
                c.step(dve.tensor_tensor(tiles(src[:, :]), hi, mid, ALU.add))
                c.wait()
                c.step(dve.tensor_tensor(tiles(src[:, :]), tiles(src[:, :]), lo, ALU.add))

            dve.wait_ge(sums_ready, 1)
            dve.tensor_reduce(wrong[:, :], ps_pack[0:1, 0:ALL], AX.X, ALU.max,
                              apply_absolute_value=True).then_inc(checked, 1)
            dve.wait_ge(checked, 4)
            dve.tensor_copy(wrong_int[:, :], wrong[:, :]).then_inc(checked, 1)
            dve.wait_ge(checked, 5)
            dve.sem_inc(checked, 1)

            dve.wait_ge(x1_ready, NB)
            with dve.Fori(0, NB) as jj:
                J = 7 - jj
                with dve.Fori(0, jj + 1) as m:
                    for h in range(2):
                        expand(J, 7 - m, h, at_two(jj) + m * 2 + h)
                for h in range(2):
                    save_acc(h, at_two(jj) + jj * 2 + (h + 1), range(3),
                             lambda: dve.wait_ge(x2_ready, jj + 1))
                c = Chain(jj * C2A + CH_2A)
                base = jj * USES_2A + EPI_2A
                own_features(c, part(J, YHI), part(J, YMID), part(J, YLO))
                turned(c, base, 0)
                turned(c, base + 1, 1)
                for n in range(2):
                    dve.wait_ge(epi_filled, base + (3 + n))
                    cols = slice(4 * n * D, (4 * n + 4) * D)
                    ps = ps_epi[:, :].rearrange("p (t c) -> p t c", t=4)
                    c.step(dve.tensor_tensor(tiles(z[:, cols]), ps[:, :, 0:D], tiles(zpart[:, J, cols]), ALU.add))
                    c.wait()
                    c.step(dve.tensor_copy(tiles(zpart[:, J, cols]), ps[:, :, D:2 * D]))
                    c.wait()
                    dve.sem_inc(epi_drained, 1)
                dve.sem_inc(z_ready, 1)

            dve.wait_ge(x2_ready, NB + 1)
            with dve.Fori(0, NB) as J:
                with dve.Fori(0, J + 1) as I:
                    for h in range(2):
                        expand(J, I, h, at_three(J) + I * 2 + h)
                for h in range(2):
                    save_acc(h, at_three(J) + J * 2 + (h + 1), range(2), lambda: None)
                c = Chain(J * C2B + CH_2B)
                base = J * USES_2B + EPI_2B
                own_features(c, part(J, XHI), part(J, XMID), part(J, XLO))
                turned(c, base, 0)
                turned(c, base + 1, 1)
                dve.wait_ge(epi_filled, base + 3)
                pass_wait(dve)
                with dve.If(J > 0):
                    dve.wait_ge(out_stored, J * 16)
                    pass_wait(dve)
                c.step(dve.tensor_tensor(z[:, :], ps_epi[:, :], zpart[:, J, :], ALU.add))
                c.wait()
                dve.sem_inc(epi_drained, 1)
                dve.sem_inc(z_ready, 1)
                own_features(c, part(J, YHI), part(J, YMID), part(J, YLO))
                c.wait()
                dve.wait_ge(tanh_done, J + (NB + 1))
                c.step(dve.tensor_tensor(z[:, :], z[:, :], src[:, :], ALU.add))
                layernorm(c, None)
                variance(c)
                scale(c, J + (2 * NB + 1))
                dve.sem_inc(out_ready, 1)

            with dve.If(unless_binary(dve) > 0):
                dve.wait_ge(product_done, ALL + TWO_A + NB * (NB + 1))
                dve.wait_ge(out_stored, 16 * NB)
                dve.sem_inc(saved_chunk, 1)
                for L in range(3):
                    dve.memset(features[L][:, :, D:D + 1], 1.0).then_inc(steps, 1)

                class General:
                    def __init__(self, base):
                        self.base, self.count = base, 0

                    def step(self, ins):
                        ins.then_inc(steps, 1)
                        self.count += 1
                        dve.wait_ge(steps, self.base + self.count)
                        pass_wait(dve)

                zt, own, square = z[:, 0:D], src[:, 0:D], agg[2][:, 0:D]

                def general_norm(g, powers):
                    g.step(dve.tensor_reduce(mean[:, 0:1], zt, AX.X, ALU.add))
                    g.step(dve.tensor_scalar(mean[:, 0:1], mean[:, 0:1], -1.0 / D, None, ALU.mult))
                    g.step(dve.tensor_scalar(zt, zt, mean[:, 0:1], None, ALU.add))
                    g.step(dve.tensor_tensor(square, zt, zt, ALU.mult))
                    g.step(dve.tensor_reduce(stat[:, 0:1], square, AX.X, ALU.add))
                    g.step(dve.tensor_scalar(stat[:, 0:1], stat[:, 0:1], 1.0 / D, LN_EPS, ALU.mult, ALU.add))
                    dve.wait_ge(rooted, powers)
                    pass_wait(dve)
                    g.step(dve.tensor_scalar(zt, zt, root[:, 0:1], None, ALU.mult))

                for L in range(3):
                    with dve.Fori(0, NT) as J:
                        m = J + L * NT
                        for c in range(CHUNKS):
                            dve.wait_ge(turned_chunk, m * CHUNKS + (c + 3))
                            dve.wait_ge(added_chunk, m * CHUNKS + (c + 1))
                            pass_wait(dve)
                            dve.tensor_copy(agg[0][:, :], acc[0][:, :, :].rearrange("p b n -> p (b n)")
                                            ).then_inc(saved_chunk, 1)
                        g = General(J * GC[L] + g_base[L])
                        dve.wait_ge(added_chunk, m * CHUNKS + (CHUNKS + 1))
                        pass_wait(dve)
                        if L == 2:
                            dve.wait_ge(stored, J * 16 + 16)
                            pass_wait(dve)
                        g.step(dve.tensor_copy(z[:, 0:D + 1], ps_epi[:, 0:D + 1]))
                        g.step(dve.tensor_copy(own, features[L][:, J, 0:D]))
                        dve.wait_ge(small_done, m * 2 + 1)
                        pass_wait(dve)
                        g.step(dve.tensor_copy(featT[:, 0:2 * P], ps_pack[0:D, 0:2 * P]))
                        if L == 0:
                            g.step(dve.tensor_scalar(rdeg[:, 0:1], z[:, D:D + 1], 1.0, 1.0, ALU.add, ALU.max))
                            g.step(dve.reciprocal(rdeg[:, 0:1], rdeg[:, 0:1]))
                            dve.wait_ge(small_done, m * 2 + 2)
                            pass_wait(dve)
                            g.step(dve.tensor_scalar(zt, acc[1][:, 0, 0:D], rdeg[:, 0:1], None, ALU.mult))
                            g.step(dve.tensor_tensor(zt, zt, acc[1][:, 0, 2 * D:3 * D], ALU.add))
                            g.step(dve.tensor_tensor(zt, zt, bias[:, :], ALU.add))
                            g.step(dve.tensor_scalar(zt, zt, 0.0, None, ALU.max))
                            g.step(dve.tensor_tensor(square, zt, zt, ALU.mult))
                            g.step(dve.tensor_reduce(stat[:, 0:1], square, AX.X, ALU.add))
                            g.step(dve.tensor_scalar(stat[:, 0:1], stat[:, 0:1], L2_EPS ** 2, None, ALU.max))
                            dve.wait_ge(rooted, J * 2 + 1)
                            pass_wait(dve)
                            g.step(dve.tensor_scalar(zt, zt, root[:, 0:1], None, ALU.mult))
                            g.step(dve.tensor_tensor(zt, zt, own, ALU.add))
                            general_norm(g, J * 2 + 2)
                            g.step(dve.tensor_copy(features[1][:, J, 0:D], zt))
                        else:
                            dve.wait_ge(small_done, m * 2 + 2)
                            pass_wait(dve)
                            g.step(dve.tensor_copy(zt, acc[1][:, 0, 0:D]))
                            dve.wait_ge(tanned, J + ((L - 1) * NT + 1))
                            pass_wait(dve)
                            if L == 1:
                                g.step(dve.tensor_copy(features[2][:, J, 0:D], zt))
                            else:
                                g.step(dve.tensor_tensor(zt, zt, features[1][:, J, 0:D], ALU.add))
                                general_norm(g, J + (2 * NT + 1))
                        assert g.count == GC[L]


def kernel(x, adj, L0_gnn_W, L0_gnn_b, L1_gnn_W):
    import numpy as np
    import concourse.bacc as bacc
    from concourse.bass_utils import run_bass_kernel_spmd

    nc = bacc.Bacc("TRN2", target_bir_lowering=False, num_devices=1)
    given = {"x": x, "adj": adj, "L0_gnn_W": L0_gnn_W, "L0_gnn_b": L0_gnn_b, "L1_gnn_W": L1_gnn_W}
    arrays = {f"in_{name}": np.ascontiguousarray(a) for name, a in given.items()}
    ins = [nc.dram_tensor(name, a.shape, mybir.dt.from_np(a.dtype), kind="ExternalInput").ap()
           for name, a in arrays.items()]
    out = nc.dram_tensor("out", (N, D), F32, kind="ExternalOutput").ap()
    gnn_kernel(nc, *ins, out)
    return run_bass_kernel_spmd(nc, [arrays], core_ids=[0]).results[0]["out"]
```

```python
from contextlib import ExitStack

import concourse.bass as bass
from concourse import mybir

ALU = mybir.AluOpType
ACT = mybir.ActivationFunctionType
AX = mybir.AxisListType
F32 = mybir.dt.float32
BF16 = mybir.dt.bfloat16
F8 = mybir.dt.float8e4
U8 = mybir.dt.uint8
U32 = mybir.dt.uint32

P = 128
N = 8192
D = 64
BLK = 1024
NB = N // BLK
TB = BLK // P
HALF = BLK // 2
QH = TB // 2
NW = BLK // 16
STEPS = 2 * NB
ALL = STEPS * NB
TWO_A = NB * (NB + 1)

XHI, XMID, XLO, YLO, YHI, YMID, PARTS = 0, 64, 128, 192, 256, 320, 384
GROUPS = 3

ORDER_LOW = [7, 6, 5, 4, 3, 2, 1, 0]
ORDER_HIGH = [7, 0, 1, 2, 6, 5, 4, 3]

USES_1, USES_2A, USES_2B = 6, 4, 3
LN_EPS = 1e-5
L2_EPS = 1e-12


def gnn_kernel(nc, x, adj, w0, b0, w1, out):
    adj_t = adj.rearrange("(j q p) (i c) -> j i p q c", q=TB, p=P, c=BLK)
    x_t = x.rearrange("(j t p) d -> j p t d", t=TB, p=P)
    out_t = out.rearrange("(j t p) d -> j p t d", t=TB, p=P)

    with ExitStack() as ctx:
        def sb(name, shape, dt):
            return ctx.enter_context(nc.sbuf_tensor(name, shape, dt))

        def psum(name, shape, dt):
            return ctx.enter_context(nc.psum_tensor(name, shape, dt))

        def sem(name):
            return ctx.enter_context(nc.semaphore(name))

        packed = sb("packed", [P, NB * NB * 2 * TB * NW], U8)
        raw = sb("raw", [P, 4, 2 * BLK], F32)
        marks = sb("marks", [P, 2, QH, BLK], F8)
        planes = sb("planes", [P, 2, TB, HALF], F8)
        feats = sb("feats", [P, N // P, PARTS], BF16)
        zpart = sb("zpart", [P, NB, TB * D], F32)
        agg = [sb(f"agg{g}", [P, BLK], F32) for g in range(GROUPS)]
        featT = sb("featT", [D, BLK], F32)
        src = sb("src", [P, TB * D], F32)
        z = sb("z", [P, TB * D], F32)
        stage = sb("stage", [P, TB, 2 * P], BF16)
        sq = agg[0][:, 0:TB * D]
        rest = agg[1][:, 0:TB * D]
        xin = agg[2][:, 0:TB * D]
        nonzero = sb("nonzero", [P, NB * TB, NB], F32)
        ring = raw[:, :, :].rearrange("p u c -> p (u c)").bitcast(F8).rearrange(
            "p (i h a c) -> p i h a c", i=4, h=2, a=TB)
        packsum = sb("packsum", [P, ALL], F32)
        pow2 = sb("pow2", [P, QH, NW], BF16)
        ident = sb("ident", [P, P], F32)
        bias = sb("bias", [P, D], F32)
        w_self = sb("w_self", [D, 3 * D], F32)
        w_a0 = sb("w_a0", [P, D], F32)
        w_a1 = sb("w_a1", [P, 2 * D], F32)
        w_y = sb("w_y", [P, D], F32)
        w_b1 = sb("w_b1", [P, 2 * D], F32)
        w_x2 = sb("w_x2", [P, D], F32)
        w_y_self = sb("w_y_self", [D, D], F32)
        w_x2_self = sb("w_x2_self", [D, D], F32)
        rdeg = sb("rdeg", [P, TB], F32)
        mean = sb("mean", [P, TB], F32)
        stat = sb("stat", [P, TB], F32)
        root = sb("root", [P, TB], F32)
        minus_half = sb("minus_half", [P, TB], F32)
        ones = sb("ones", [P, 1], F32)
        worth = sb("worth", [P, QH], F32)
        wrong = sb("wrong", [1, 1], F32)
        wrong_int = sb("wrong_int", [1, 1], mybir.dt.int32)

        general = packed[:, :].bitcast(F32)
        each = N // P * (D + 1)
        features = [general[:, n * each:(n + 1) * each].rearrange("p (t d) -> p t d", d=D + 1) for n in range(3)]

        acc = [psum(f"acc{g}", [P, 2, HALF], F32) for g in range(GROUPS)]
        ps_pack = psum("ps_pack", [P, HALF], F32)
        ps_epi = psum("ps_epi", [P, HALF], F32)

        consts = sem("consts")
        zeroed = sem("zeroed")
        weights_landed = sem("weights_landed")
        raw_landed = [sem(f"raw_landed{u}") for u in range(4)]
        marked = sem("marked")
        counted = sem("counted")
        pack_done = sem("pack_done")
        pack_saved = sem("pack_saved")
        planes_ready = sem("planes_ready")
        product_done = sem("product_done")
        acc_saved = sem("acc_saved")
        xin_landed = sem("xin_landed")
        split = sem("split")
        x_ready = sem("x_ready")
        x1_ready = sem("x1_ready")
        x2_ready = sem("x2_ready")
        src_landed = sem("src_landed")
        src_read = sem("src_read")
        epi_filled = sem("epi_filled")
        epi_drained = sem("epi_drained")
        chain = sem("chain")
        stat_ready = sem("stat_ready")
        root_ready = sem("root_ready")
        y_ready = sem("y_ready")
        staged = sem("staged")
        z_ready = sem("z_ready")
        tanh_done = sem("tanh_done")
        out_ready = sem("out_ready")
        out_stored = sem("out_stored")
        sums_ready = sem("sums_ready")
        checked = sem("checked")
        x_landed = sem("x_landed")
        chunk_landed = [sem(f"chunk_landed{n}") for n in range(2)]
        turned_chunk = sem("turned_chunk")
        saved_chunk = sem("saved_chunk")
        added_chunk = sem("added_chunk")
        small_done = sem("small_done")
        steps = sem("steps")
        rooted = sem("rooted")
        tanned = sem("tanned")
        stored = sem("stored")
        passed = sem("passed")

        def pass_wait(eng):
            eng.sem_inc(passed, 1)

        def tiles(ap):
            return ap.rearrange("p (t d) -> p t d", d=D)

        def spread(ap):
            return ap.unsqueeze(2).to_broadcast([P, TB, D])

        def part(J, col):
            return feats[:, bass.ds(J * TB, TB), col:col + D]

        def bytes_of(J, I, h):
            width = TB * NW
            return packed[:, bass.ds(((J * NB + I) * 2 + h) * width, width)]

        def words_of(J, I, h):
            width = TB * NW
            ap = packed[:, bass.ds(((J * NB + I) * 2 + h) * width, width)].bitcast(U32)
            return ap.rearrange("p (a n) -> p a n", a=TB)

        def at_one(J):
            return J * STEPS

        def at_two(jj):
            return jj * (jj + 1) + ALL

        def at_three(jj):
            return (jj * (17 - jj) & 127) + (ALL + TWO_A)

        C1, C2A, C2B = 30, 8, 15
        EPI_2A = USES_1 * NB
        EPI_2B = EPI_2A + USES_2A * NB
        CH_2A = C1 * NB
        CH_2B = CH_2A + C2A * NB

        CONSTS = 6 + 2 * QH
        WEIGHTS = 16 * 15

        GC = [22, 5, 12]
        CHECK = 6
        NT = N // P
        CHUNKS = N // BLK
        g_base = [3, 3 + GC[0] * NT, 3 + (GC[0] + GC[1]) * NT]

        def unless_binary(eng):
            eng.wait_ge(checked, CHECK)
            return eng.value_load(wrong_int[:, :], min_val=0, max_val=1 << 24)

        block = ctx.enter_context(nc.Block())

        @block.sync
        def _(sp):
            def load_step(J, I, n, first):
                for u in range(4):
                    if not first:
                        sp.wait_ge(counted, 4 * n + (u - 3))
                        pass_wait(sp)
                    sp.dma_start(raw[:, u, :].rearrange("p (q c) -> p q c", q=2),
                                 adj_t[J, I, :, 2 * u:2 * u + 2, :]).then_inc(raw_landed[u], 16)

            def load_block(J, order, first=False):
                for k, I in enumerate(order):
                    load_step(J, I, J * NB + k, first and k == 0)
                    if k == 5:
                        if not first:
                            sp.wait_ge(src_read, J)
                        sp.dma_start(tiles(src[:, :]), x_t[J]).then_inc(src_landed, 16)

            load_block(0, ORDER_LOW, first=True)
            with sp.Fori(1, 4) as J:
                load_block(J, ORDER_LOW)
            with sp.Fori(4, NB) as J:
                load_block(J, ORDER_HIGH)
            with sp.Fori(0, NB) as J:
                sp.wait_ge(out_ready, J + 1)
                pass_wait(sp)
                sp.dma_start(out_t[7 - J], tiles(z[:, :])).then_inc(out_stored, 16)
            sp.wait_ge(out_stored, 16 * NB)

            with sp.If(unless_binary(sp) > 0):
                sp.wait_ge(product_done, ALL + TWO_A + NB * (NB + 1))
                sp.sem_inc(stored, 16)
                sp.dma_start(features[0][:, :, 0:D], x.rearrange("(t p) d -> p t d", p=P)).then_inc(x_landed, 16)
                for L in range(3):
                    with sp.Fori(0, NT) as J:
                        m = J + L * NT
                        for c in range(CHUNKS):
                            sp.wait_ge(turned_chunk, m * CHUNKS + (c + 1))
                            pass_wait(sp)
                            sp.dma_start(raw[:, c % 2, 0:BLK], adj[bass.ds(J * P, P), c * BLK:(c + 1) * BLK]
                                         ).then_inc(chunk_landed[c % 2], 16)
                        if L == 2:
                            sp.wait_ge(steps, J * GC[2] + (g_base[2] + GC[2]))
                            pass_wait(sp)
                            sp.dma_start(out[bass.ds(J * P, P), :], z[:, 0:D]).then_inc(stored, 16)
                sp.wait_ge(stored, 16 * (NT + 1))

        @block.scalar
        def _(act):
            act.wait_ge(zeroed, 3)
            for dst, src_ap in [
                (w_self[:, 0:D], w0[D:2 * D, :]), (w_self[:, 2 * D:3 * D], w0[0:D, :]),
                (w_a0[0:D, :], w0[D:2 * D, :]), (w_a0[D:P, :], w0[D:2 * D, :]),
                (w_a1[0:D, 0:D], w0[D:2 * D, :]), (w_a1[D:P, D:2 * D], w1[0, 0:D, :]),
                (w_y[0:D, :], w1[0, 0:D, :]), (w_y[D:P, :], w1[0, 0:D, :]),
                (w_b1[0:D, D:2 * D], w1[1, 0:D, :]), (w_b1[D:P, 0:D], w1[0, 0:D, :]),
                (w_x2[0:D, :], w1[1, 0:D, :]), (w_x2[D:P, :], w1[1, 0:D, :]),
                (w_y_self[:, :], w1[0, D:2 * D, :]), (w_x2_self[:, :], w1[1, D:2 * D, :]),
                (bias[:, :], b0.rearrange("(a d) -> a d", a=1).to_broadcast([P, D])),
            ]:
                act.dma_start(dst, src_ap).then_inc(weights_landed, 16)

            def count_block(J, order):
                for k, I in enumerate(order):
                    for u in range(4):
                        act.wait_ge(marked, J * 4 * NB + (4 * k + u + 1))
                        for q in range(2):
                            words = raw[:, u, q * BLK:(q + 1) * BLK]
                            ins = act.activation(words, words.bitcast(U32), ACT.Sign,
                                                 accum_out=nonzero[:, bass.ds(J * TB + (2 * u + q), 1), I])
                        ins.then_inc(counted, 1)

            with act.Fori(0, 4) as J:
                count_block(J, ORDER_LOW)
            with act.Fori(4, NB) as J:
                count_block(J, ORDER_HIGH)
            with act.Fori(0, 2 * NB) as n:
                act.wait_ge(z_ready, n + 1)
                act.activation(z[:, :], z[:, :], ACT.Tanh).then_inc(tanh_done, 1)

            with act.If(unless_binary(act) > 0):
                for L in (1, 2):
                    with act.Fori(0, NT) as J:
                        act.wait_ge(steps, J * GC[L] + (g_base[L] + 4))
                        act.activation(z[:, 0:D], z[:, 0:D], ACT.Tanh).then_inc(tanned, 1)

        @block.gpsimd
        def _(pool):
            pool.memset(w_self[:, :], 0.0).then_inc(zeroed, 1)
            pool.memset(w_a1[:, :], 0.0).then_inc(zeroed, 1)
            pool.memset(w_b1[:, :], 0.0).then_inc(zeroed, 1)
            pool.memset(pow2[:, :, :], 0.0).then_inc(consts, 1)
            pool.memset(ident[:, :], 0.0).then_inc(consts, 1)
            pool.memset(minus_half[:, :], -0.5).then_inc(consts, 1)
            pool.memset(feats[:, :, YLO:YLO + D], 0.0).then_inc(consts, 1)
            pool.memset(feats[:, :, YHI:YHI + 2 * D], 0.0).then_inc(consts, 1)
            pool.wait_ge(consts, 5)
            pool.affine_select(out=ident[:, :], in_=ident[:, :], compare_op=ALU.not_equal, fill=1.0,
                               base=0, pattern=[[-1, P]], channel_multiplier=1).then_inc(consts, 1)
            for q in range(QH):
                for half in range(2):
                    pool.wait_ge(consts, 6 + 2 * q + half)
                    pool.affine_select(out=pow2[:, q, :], in_=pow2[:, q, :], compare_op=ALU.not_equal,
                                       fill=float(2 ** (2 * q + half)) / 2, base=-half * NW,
                                       pattern=[[-1, NW]], channel_multiplier=1).then_inc(consts, 1)

            def split_feats(J, ap, col, lo, count, base, done):
                pool.tensor_copy(part(J, col), tiles(ap)).then_inc(split, 1)
                pool.wait_ge(split, count * 4 + (base + 1))
                pass_wait(pool)
                pool.tensor_tensor(tiles(rest), tiles(ap), part(J, col), ALU.subtract).then_inc(split, 1)
                pool.wait_ge(split, count * 4 + (base + 2))
                pool.tensor_copy(part(J, col + D), tiles(rest)).then_inc(split, 1)
                pool.wait_ge(split, count * 4 + (base + 3))
                pass_wait(pool)
                pool.tensor_tensor(part(J, lo), tiles(rest), part(J, col + D), ALU.subtract).then_inc(split, 1)
                pool.wait_ge(split, count * 4 + (base + 4))
                pool.sem_inc(done, 1)

            def power(n):
                pool.wait_ge(stat_ready, n)
                pool.tensor_tensor(root[:, :], stat[:, :], minus_half[:, :], ALU.pow).then_inc(root_ready, 1)

            for k, I in enumerate(ORDER_LOW):
                pool.dma_start(tiles(xin), x_t[I]).then_inc(xin_landed, 16)
                pool.wait_ge(xin_landed, 16 * (k + 1))
                split_feats(I, xin, XHI, XLO, k, 0, x_ready)

            def epilogue_one(J):
                power(J * 2 + 1)
                power(J * 2 + 2)
                pool.wait_ge(y_ready, J + 1)
                split_feats(J, z[:, :], YHI, YLO, J, 4 * NB, x1_ready)

            with pool.Fori(0, NB - 1) as J:
                epilogue_one(J)
            pool.wait_ge(product_done, ALL)
            pool.memset(feats[:, :, XHI:XLO + D], 0.0).then_inc(x2_ready, 1)
            epilogue_one(NB - 1)
            with pool.Fori(0, NB) as jj:
                pool.wait_ge(tanh_done, jj + 1)
                pass_wait(pool)
                split_feats(7 - jj, z[:, :], XHI, XLO, jj, 8 * NB, x2_ready)
            with pool.Fori(0, NB) as J:
                power(J + (2 * NB + 1))

            with pool.If(unless_binary(pool) > 0):
                def general_power(value):
                    pool.wait_ge(steps, value)
                    pool.tensor_tensor(root[:, 0:1], stat[:, 0:1], minus_half[:, 0:1], ALU.pow).then_inc(rooted, 1)

                with pool.Fori(0, NT) as J:
                    general_power(J * GC[0] + (g_base[0] + 12))
                    general_power(J * GC[0] + (g_base[0] + 20))
                with pool.Fori(0, NT) as J:
                    general_power(J * GC[2] + (g_base[2] + 11))

        @block.tensor
        def _(pe):
            def pack(J, s):
                h = s % 2
                pe.wait_ge(marked, J * (2 * STEPS) + (2 * s + 2))
                if not (isinstance(J, int) and s == 0):
                    pe.wait_ge(pack_saved, J * STEPS + s)
                pe.wait_ge(consts, CONSTS)
                pass_wait(pe)
                for a in range(TB):
                    for q in range(QH):
                        mm = pe.matmul(ps_pack[:, a * NW:(a + 1) * NW], marks[:, h, q, a * P:(a + 1) * P],
                                       pow2[:, q, :], start=q == 0, stop=q == QH - 1)
                mm.then_inc(pack_done, 1)

            def multiply(I, h, groups, start, moving=planes, stationary=None, opens=()):
                pass_wait(pe)
                for a in range(TB):
                    for g in groups:
                        own = feats[:, I * TB + a, g * P:(g + 1) * P] if stationary is None else stationary(a, g)
                        mm = pe.matmul(acc[g][:, h, :], own, moving[:, h, a, :],
                                       start=(start or g in opens) and a == 0, stop=a == TB - 1,
                                       skip_group_check=True)
                return mm

            def turn(use, half):
                pe.wait_ge(epi_drained, use)
                pe.wait_ge(consts, CONSTS)
                pass_wait(pe)
                for t in range(4):
                    tile = 4 * half + t
                    mm = pe.transpose(ps_epi[0:D, t * P:(t + 1) * P], src[:, tile * D:(tile + 1) * D],
                                      ident[:, :])
                mm.then_inc(epi_filled, 1)

            def weigh(use, first_tile, count, products, width):
                pe.wait_ge(epi_drained, use)
                pe.wait_ge(weights_landed, WEIGHTS)
                pass_wait(pe)
                for t in range(count):
                    rows = slice((first_tile + t) * P, (first_tile + t + 1) * P)
                    for n, (lhs, w, col) in enumerate(products):
                        at = t * width + col
                        mm = pe.matmul(ps_epi[:, at:at + w.shape[1]], lhs[:, rows], w, start=n == 0,
                                       stop=n == len(products) - 1, skip_group_check=True)
                mm.then_inc(epi_filled, 1)

            own = featT[:, :]
            ONE = [(own, w_self[:, :], 0), (agg[0], w_a0[:, :], 0), (agg[1], w_a1[:, :], 0), (agg[2], w_y[:, :], D)]
            TWO = [(agg[1], w_b1[:, :], 0), (agg[2], w_y[:, :], 0), (own, w_y_self[:, :], 0), (agg[0], w_x2[:, :], D)]
            THREE = [(agg[0], w_x2[:, :], 0), (agg[1][0:D, :], w_x2[0:D, :], 0), (own, w_x2_self[:, :], 0)]

            def epilogue_one(J, piece):
                base = J * USES_1
                if piece == 0:
                    pe.wait_ge(src_landed, J * 16 + 16)
                    turn(base, 0)
                elif piece == 1:
                    turn(base + 1, 1)
                elif piece == 2:
                    pe.wait_ge(acc_saved, J * 2 + 2)
                    weigh(base + 2, 0, 2, ONE, 3 * D)
                    weigh(base + 3, 2, 2, ONE, 3 * D)
                else:
                    weigh(base + 4, 4, 2, ONE, 3 * D)
                    weigh(base + 5, 6, 2, ONE, 3 * D)

            def block_one(J, order, first=False, last=False):
                for s in range(STEPS):
                    k, h = divmod(s, 2)
                    I = order[k]
                    if not (last and s == STEPS - 1):
                        pack(J, s + 1)
                    pe.wait_ge(planes_ready, J * STEPS + (s + 1))
                    if k == 0 and not first:
                        pe.wait_ge(acc_saved, J * 2 + (h - 1))
                    pe.wait_ge(x_ready, k + 1 if first else NB)
                    ends = k in (0, NB - 1)
                    if not (first or ends):
                        with pe.If(J > I):
                            pe.wait_ge(x1_ready, I + 1)
                            multiply(I, h, [2], False)
                    if k == NB - 1 and not first:
                        pe.wait_ge(x1_ready, I + 1)
                    multiply(I, h, range(3) if ends else range(2), k == 0).then_inc(product_done, 1)
                    if not first and s < 4:
                        epilogue_one(J - 1, s)

            pack(0, 0)
            block_one(0, ORDER_LOW, first=True)
            with pe.Fori(1, 4) as J:
                block_one(J, ORDER_LOW)
            with pe.Fori(4, NB - 1) as J:
                block_one(J, ORDER_HIGH)
            block_one(NB - 1, ORDER_HIGH, last=True)
            for piece in range(4):
                epilogue_one(NB - 1, piece)

            pe.wait_ge(pack_saved, ALL)
            pe.wait_ge(counted, 2 * ALL)
            pe.wait_ge(checked, 3)
            pe.matmul(ps_pack[0:1, 0:ALL], ones[:, :], packsum[:, :], start=True, stop=False)
            counts = nonzero[:, :, :].rearrange("p (j h q) i -> p q j i h", j=NB, h=2)
            for q in range(QH):
                mm = pe.matmul(ps_pack[0:1, 0:ALL], worth[:, q:q + 1], counts[:, q], start=False, stop=q == QH - 1)
            mm.then_inc(sums_ready, 1)

            def diagonal(jj):
                for h in range(2):
                    pe.wait_ge(planes_ready, at_two(jj) + (h + 1))
                    pe.wait_ge(staged, jj + 1)
                    pe.wait_ge(acc_saved, jj * 2 + (2 * NB - 1 + h))
                    multiply(None, h, [1, 2], True,
                             stationary=lambda a, g: stage[:, a, (g - 1) * P:g * P]).then_inc(product_done, 1)

            def turn_block(use, steps_before):
                pe.wait_ge(chain, steps_before + 2)
                turn(use, 0)
                turn(use + 1, 1)

            def weigh_two(jj):
                pe.wait_ge(acc_saved, jj * 2 + (2 * NB + 2))
                weigh(jj * USES_2A + (EPI_2A + 2), 0, 4, TWO, 2 * D)
                weigh(jj * USES_2A + (EPI_2A + 3), 4, 4, TWO, 2 * D)

            def weigh_three(jj):
                pe.wait_ge(acc_saved, jj * 2 + (4 * NB + 2))
                weigh(jj * USES_2B + (EPI_2B + 2), 0, 8, THREE, D)

            pe.wait_ge(x2_ready, 1)
            diagonal(0)
            turn_block(EPI_2A, CH_2A)
            with pe.Fori(1, NB) as jj:
                diagonal(jj)
                weigh_two(jj - 1)
                for I in range(NB - 1, 0, -1):
                    with pe.If(jj > 7 - I):
                        for h in range(2):
                            pe.wait_ge(planes_ready, at_two(jj) + (2 * (7 - I) + h + 3))
                            pe.wait_ge(x2_ready, 9 - I)
                            multiply(I, h, range(3), False, ring[:, I % 4],
                                     opens=[0] if I == NB - 1 else []).then_inc(product_done, 1)
                    if I == NB - 1:
                        turn_block(jj * USES_2A + EPI_2A, jj * C2A + CH_2A)

            def lower(jj, I, opens):
                for h in range(2):
                    done = at_three(jj + 1) - 2 if I == 0 else at_three(jj) + 2 * (I - 1)
                    pe.wait_ge(planes_ready, done + (h + 1))
                    if opens:
                        pe.wait_ge(acc_saved, jj * 2 + (4 * NB - 1 + h))
                    if I == 0:
                        pe.wait_ge(x2_ready, NB + 1)
                    multiply(I, h, range(2), opens, ring[:, (I + 2) % 4] if I else planes).then_inc(product_done, 1)

            lower(0, 1, True)
            weigh_two(NB - 1)
            lower(0, 2, False)
            turn_block(EPI_2B, CH_2B)
            for I in range(3, NB):
                lower(0, I, False)
            lower(0, 0, False)
            with pe.Fori(1, NB - 1) as jj:
                lower(jj, 1, True)
                weigh_three(jj - 1)
                for I in range(2, NB - 1):
                    with pe.If(jj < 8 - I):
                        lower(jj, I, False)
                    if I == 2:
                        turn_block(jj * USES_2B + EPI_2B, jj * C2B + CH_2B)
                lower(jj, 0, False)
            lower(NB - 1, 0, True)
            weigh_three(NB - 2)
            turn_block((NB - 1) * USES_2B + EPI_2B, (NB - 1) * C2B + CH_2B)
            weigh_three(NB - 1)

            with pe.If(unless_binary(pe) > 0):
                pe.sem_inc(turned_chunk, 2)
                pe.sem_inc(added_chunk, 1)
                pe.wait_ge(x_landed, 16)
                for L in range(3):
                    with pe.Fori(0, NT) as J:
                        m = J + L * NT
                        for c in range(CHUNKS):
                            pe.wait_ge(chunk_landed[c % 2], m * (16 * CHUNKS // 2) + 16 * (c // 2 + 1))
                            pass_wait(pe)
                            if L == 0 and c == 0:
                                pe.wait_ge(steps, 3)
                            pe.wait_ge(saved_chunk, m * CHUNKS + (c + 1))
                            pass_wait(pe)
                            for a in range(TB):
                                mm = pe.transpose(acc[0][:, a // 4, (a % 4) * P:(a % 4 + 1) * P],
                                                  raw[:, c % 2, a * P:(a + 1) * P], ident[:, :])
                            mm.then_inc(turned_chunk, 1)
                            pe.wait_ge(saved_chunk, m * CHUNKS + (c + 2))
                            pass_wait(pe)
                            for a in range(TB):
                                mm = pe.matmul(ps_epi[:, 0:D + 1], agg[0][:, a * P:(a + 1) * P],
                                               features[L][:, c * TB + a, :], start=c + a == 0,
                                               stop=c == CHUNKS - 1 and a == TB - 1)
                            mm.then_inc(added_chunk, 1)
                        at = J * GC[L] + g_base[L]
                        pe.wait_ge(steps, at + 2)
                        pass_wait(pe)
                        pe.transpose(ps_pack[0:D, 0:P], z[:, 0:D], ident[:, :])
                        pe.transpose(ps_pack[0:D, P:2 * P], src[:, 0:D], ident[:, :]).then_inc(small_done, 1)
                        pe.wait_ge(steps, at + 3)
                        pass_wait(pe)
                        if L == 0:
                            pe.matmul(acc[1][:, 0, 0:3 * D], featT[:, P:2 * P], w_self[:, :], start=True, stop=True)
                            pe.matmul(acc[1][:, 0, 0:D], featT[:, 0:P], w_a0[0:D, :], start=False, stop=True,
                                      skip_group_check=True).then_inc(small_done, 1)
                        else:
                            w, w_own = (w_y, w_y_self) if L == 1 else (w_x2, w_x2_self)
                            pe.matmul(acc[1][:, 0, 0:D], featT[:, P:2 * P], w_own[:, :], start=True, stop=False)
                            pe.matmul(acc[1][:, 0, 0:D], featT[:, 0:P], w[0:D, :], start=False,
                                      stop=True).then_inc(small_done, 1)

        @block.vector
        def _(dve):
            def mark(J, s, first=False):
                k, h = divmod(s, 2)
                for u in (2 * h, 2 * h + 1):
                    dve.wait_ge(raw_landed[u], J * (16 * NB) + 16 * (k + 1))
                    if not first:
                        dve.wait_ge(pack_done, J * STEPS + (s - 1))
                    out_ap = marks[:, h, 2 * (u % 2):2 * (u % 2) + 2, :].rearrange("p q c -> p (q c)")
                    dve.tensor_scalar(out_ap.bitcast(U8), raw[:, u, :], 1.0, 64.0, ALU.is_equal,
                                      ALU.mult).then_inc(marked, 1)

            def save_pack(J, s, I):
                dve.wait_ge(pack_done, J * STEPS + (s + 1))
                dve.tensor_scalar(bytes_of(J, I, s % 2), ps_pack[:, :], 1.0, None, ALU.mult, ALU.add,
                                  accum_out=packsum[:, bass.ds((J * NB + I) * 2 + s % 2, 1)]).then_inc(pack_saved, 1)

            def expand(J, I, h, used, wide=None):
                if used is not None:
                    dve.wait_ge(product_done, used)
                    pass_wait(dve)
                words = words_of(J, I, h)
                wide = planes[:, h, :, :].bitcast(U32) if wide is None else wide
                for bit in range(8):
                    shift, op = (6 - bit, ALU.logical_shift_left) if bit < 7 else (1, ALU.logical_shift_right)
                    ins = dve.tensor_scalar(wide[:, :, bit * NW // 4:(bit + 1) * NW // 4], words, shift,
                                            0x40404040, op, ALU.bitwise_and)
                ins.then_inc(planes_ready, 1)

            def save_acc(h, done, groups):
                dve.wait_ge(product_done, done)
                pass_wait(dve)
                for g in groups:
                    ins = dve.tensor_scalar(agg[g][:, h * HALF:(h + 1) * HALF], acc[g][:, h, :], 0.5, None, ALU.mult)
                ins.then_inc(acc_saved, 1)

            class Chain:
                def __init__(self, base, count=0):
                    self.base, self.count = base, count

                def wait(self):
                    dve.wait_ge(chain, self.base + self.count)
                    pass_wait(dve)

                def step(self, ins):
                    ins.then_inc(chain, 1)
                    self.count += 1

            def turned(c, use, half):
                dve.wait_ge(epi_filled, use + 1)
                pass_wait(dve)
                c.step(dve.tensor_copy(featT[:, half * HALF:(half + 1) * HALF], ps_epi[0:D, :]))
                c.wait()
                dve.sem_inc(epi_drained, 1)

            def layernorm(c):
                c.wait()
                c.step(dve.tensor_reduce(mean[:, :], tiles(z[:, :]), AX.X, ALU.add))
                c.wait()
                c.step(dve.tensor_scalar(mean[:, :], mean[:, :], -1.0 / D, None, ALU.mult))
                c.wait()
                c.step(dve.tensor_tensor(tiles(z[:, :]), tiles(z[:, :]), spread(mean[:, :]), ALU.add))

            def variance(c):
                c.wait()
                c.step(dve.tensor_tensor(sq, z[:, :], z[:, :], ALU.mult))
                c.wait()
                c.step(dve.tensor_reduce(stat[:, :], tiles(sq), AX.X, ALU.add))
                c.wait()
                c.step(dve.tensor_scalar(stat[:, :], stat[:, :], 1.0 / D, LN_EPS, ALU.mult, ALU.add))
                c.wait()
                dve.sem_inc(stat_ready, 1)

            def scale(c, root_count):
                dve.wait_ge(root_ready, root_count)
                c.step(dve.tensor_tensor(tiles(z[:, :]), tiles(z[:, :]), spread(root[:, :]), ALU.mult))
                c.wait()

            def epilogue_one(J, piece):
                base = J * USES_1
                if piece == 0:
                    c = Chain(J * C1, 0)
                    dve.wait_ge(counted, J * (4 * NB) + 4 * NB)
                    c.step(dve.tensor_reduce(rdeg[:, :], nonzero[:, bass.ds(J * TB, TB), :], AX.X, ALU.add))
                    c.wait()
                    c.step(dve.tensor_scalar(rdeg[:, :], rdeg[:, :], 1.0, 1.0, ALU.add, ALU.max))
                    c.wait()
                    c.step(dve.reciprocal(rdeg[:, :], rdeg[:, :]))
                    turned(c, base, 0)
                elif piece == 1:
                    turned(Chain(J * C1, 4), base + 1, 1)
                elif piece in (2, 3):
                    c = Chain(J * C1, 5 if piece == 2 else 11)
                    for n in (0, 1):
                        pair = 2 * (piece - 2) + n
                        dve.wait_ge(epi_filled, base + (3 + pair))
                        cols = slice(2 * pair * D, (2 * pair + 2) * D)
                        ps = ps_epi[:, 0:6 * D].rearrange("p (t c) -> p t c", t=2)
                        c.step(dve.tensor_copy(tiles(zpart[:, J, cols]), ps[:, :, D:2 * D]))
                        c.step(dve.tensor_tensor(tiles(z[:, cols]), ps[:, :, 0:D],
                                                 rdeg[:, 2 * pair:2 * pair + 2].unsqueeze(2).to_broadcast([P, 2, D]),
                                                 ALU.mult))
                        c.wait()
                        c.step(dve.tensor_tensor(tiles(z[:, cols]), tiles(z[:, cols]), ps[:, :, 2 * D:3 * D], ALU.add))
                        c.wait()
                        dve.sem_inc(epi_drained, 1)
                elif piece == 4:
                    c = Chain(J * C1, 17)
                    c.step(dve.tensor_tensor(tiles(z[:, :]), tiles(z[:, :]),
                                             bias[:, :].unsqueeze(1).to_broadcast([P, TB, D]), ALU.add))
                    c.wait()
                    c.step(dve.scalar_tensor_tensor(sq, z[:, :], 0.0, z[:, :], ALU.max, ALU.mult))
                    c.wait()
                    c.step(dve.tensor_reduce(stat[:, :], tiles(sq), AX.X, ALU.add))
                    c.wait()
                    c.step(dve.tensor_scalar(stat[:, :], stat[:, :], L2_EPS ** 2, None, ALU.max))
                    c.wait()
                    dve.sem_inc(stat_ready, 1)
                elif piece == 5:
                    c = Chain(J * C1, 21)
                    dve.wait_ge(root_ready, J * 2 + 1)
                    c.step(dve.scalar_tensor_tensor(tiles(z[:, :]), tiles(z[:, :]), 0.0, spread(root[:, :]),
                                                    ALU.max, ALU.mult))
                    c.wait()
                    c.step(dve.tensor_tensor(z[:, :], z[:, :], src[:, :], ALU.add))
                    c.wait()
                    dve.sem_inc(src_read, 1)
                    layernorm(c)
                elif piece == 6:
                    variance(Chain(J * C1, 26))
                else:
                    c = Chain(J * C1, 29)
                    scale(c, J * 2 + 2)
                    dve.sem_inc(y_ready, 1)

            def block_one(J, order, first=False, last=False):
                for s in range(STEPS):
                    k, h = divmod(s, 2)
                    nxt = (order + [7])[(s + 1) // 2]
                    if not (last and s + 1 >= STEPS):
                        save_pack(J, s + 1, nxt) if s + 1 < STEPS else save_pack(J + 1, 0, nxt)
                        dve.wait_ge(pack_saved, J * STEPS + (s + 2))
                        over = s + 1 >= STEPS
                        expand(J + 1 if over else J, nxt, (s + 1) % 2, None if first and s == 0 else J * STEPS + s)
                    if not (last and s + 2 >= STEPS):
                        mark(J, s + 2)
                    if not first:
                        if s < 8:
                            epilogue_one(J - 1, s)
                    if k == NB - 1:
                        dve.wait_ge(x_ready, NB) if first else dve.wait_ge(x1_ready, J)
                        save_acc(h, J * STEPS + (s + 1), range(3))

            dve.memset(ones[:, :], 1.0).then_inc(checked, 1)
            dve.wait_ge(consts, CONSTS)
            dve.tensor_reduce(worth[:, :], pow2[:, :, :], AX.X, ALU.add).then_inc(checked, 1)
            dve.wait_ge(checked, 2)
            dve.tensor_scalar(worth[:, :], worth[:, :], -2.0, None, ALU.mult).then_inc(checked, 1)
            mark(0, 0, first=True)
            mark(0, 1, first=True)
            save_pack(0, 0, 7)
            dve.wait_ge(pack_saved, 1)
            expand(0, 7, 0, None)
            block_one(0, ORDER_LOW, first=True)
            with dve.Fori(1, 4) as J:
                block_one(J, ORDER_LOW)
            with dve.Fori(4, NB - 1) as J:
                block_one(J, ORDER_HIGH)
            block_one(NB - 1, ORDER_HIGH, last=True)
            for piece in range(8):
                epilogue_one(NB - 1, piece)

            dve.wait_ge(sums_ready, 1)
            dve.tensor_reduce(wrong[:, :], ps_pack[0:1, 0:ALL], AX.X, ALU.max,
                              apply_absolute_value=True).then_inc(checked, 1)
            dve.wait_ge(checked, 4)
            dve.tensor_copy(wrong_int[:, :], wrong[:, :]).then_inc(checked, 1)
            dve.wait_ge(checked, 5)
            dve.sem_inc(checked, 1)

            ring32 = ring.bitcast(U32)

            def expand_ring(J, I, slot, n):
                for h in range(2):
                    wide = ring32[:, bass.ds(slot, 1), h].rearrange("p i a c -> p (i a) c")
                    expand(J, I, h, n + (h - 3), wide=wide)

            def own_x1(c, into):
                c.step(dve.tensor_tensor(tiles(into), part(c.J, YHI), part(c.J, YMID), ALU.add))
                c.wait()
                c.step(dve.tensor_tensor(tiles(into), tiles(into), part(c.J, YLO), ALU.add))

            def own_x2(c, into):
                c.step(dve.tensor_tensor(tiles(into), part(c.J, XHI), part(c.J, XMID), ALU.add))
                c.wait()
                c.step(dve.tensor_tensor(tiles(into), tiles(into), part(c.J, XLO), ALU.add))

            def at_block(jj, base, count, done):
                c = Chain(jj * count + base, done)
                c.J = 7 - jj
                return c

            def stage_block(jj):
                J = 7 - jj
                dve.tensor_copy(stage[:, :, :], feats[:, bass.ds(J * TB, TB), XLO:PARTS]).then_inc(staged, 1)

            def turned_two(jj):
                c = at_block(jj, CH_2A, C2A, 2)
                turned(c, jj * USES_2A + EPI_2A, 0)
                turned(c, jj * USES_2A + (EPI_2A + 1), 1)

            def weighed_two(jj):
                c = at_block(jj, CH_2A, C2A, 4)
                for n in range(2):
                    dve.wait_ge(epi_filled, jj * USES_2A + (EPI_2A + 3 + n))
                    pass_wait(dve)
                    cols = slice(4 * n * D, (4 * n + 4) * D)
                    ps = ps_epi[:, :].rearrange("p (t c) -> p t c", t=4)
                    c.step(dve.tensor_tensor(tiles(z[:, cols]), ps[:, :, 0:D], tiles(zpart[:, c.J, cols]), ALU.add))
                    c.wait()
                    c.step(dve.tensor_copy(tiles(zpart[:, c.J, cols]), ps[:, :, D:2 * D]))
                    c.wait()
                    dve.sem_inc(epi_drained, 1)
                dve.sem_inc(z_ready, 1)

            dve.wait_ge(x1_ready, NB)
            dve.wait_ge(x2_ready, 1)
            dve.wait_ge(counted, 2 * ALL)
            dve.memset(agg[0][:, :], 0.0)
            stage_block(0)
            for h in range(2):
                expand(7, 7, h, ALL - 1 + h)
            own_x1(at_block(0, CH_2A, C2A, 0), src[:, :])
            turned_two(0)

            def upper(jj, groups):
                J = 7 - jj
                dve.wait_ge(product_done, at_two(jj - 1) + 2)
                pass_wait(dve)
                stage_block(jj)
                expand(J, J, 0, None)
                expand(J, J, 1, None)
                dve.wait_ge(x2_ready, jj)
                for h in range(2):
                    save_acc(h, at_two(jj) + (h - 1), groups)
                expand_ring(J, 7, 3, at_two(jj) + 2)
                weighed_two(jj - 1)
                own_x1(at_block(jj, CH_2A, C2A, 0), src[:, :])
                if not isinstance(jj, int):
                    expand_ring(J, 6, 2, at_two(jj) + 4)
                turned_two(jj)

            upper(1, [1, 2])
            with dve.Fori(2, NB) as jj:
                upper(jj, range(3))
                with dve.If(jj > 2):
                    with dve.Fori(2, jj) as m:
                        expand_ring(7 - jj, 7 - m, (7 - m) & 3, at_two(jj) + m * 2 + 2)

            def turned_three(jj):
                c = at_block(jj, CH_2B, C2B, 2)
                turned(c, jj * USES_2B + EPI_2B, 0)
                turned(c, jj * USES_2B + (EPI_2B + 1), 1)

            def weighed_three(jj):
                c = at_block(jj, CH_2B, C2B, 4)
                dve.wait_ge(epi_filled, jj * USES_2B + (EPI_2B + 3))
                pass_wait(dve)
                dve.wait_ge(out_stored, jj * 16)
                pass_wait(dve)
                c.step(dve.tensor_tensor(z[:, :], ps_epi[:, :], zpart[:, c.J, :], ALU.add))
                c.wait()
                dve.sem_inc(epi_drained, 1)
                dve.sem_inc(z_ready, 1)
                own_x1(c, rest)
                c.wait()
                dve.wait_ge(tanh_done, jj + (NB + 1))
                pass_wait(dve)
                c.step(dve.tensor_tensor(z[:, :], z[:, :], rest, ALU.add))
                layernorm(c)
                variance(c)
                scale(c, jj + (2 * NB + 1))
                dve.sem_inc(out_ready, 1)

            expand_ring(7, 1, 3, at_three(0))
            dve.wait_ge(x2_ready, NB)
            for h in range(2):
                save_acc(h, at_three(0) + (h - 1), range(3))
            expand_ring(7, 2, 0, at_three(0) + 2)
            weighed_two(NB - 1)
            own_x2(at_block(0, CH_2B, C2B, 0), src[:, :])
            turned_three(0)
            for I in range(3, NB):
                expand_ring(7, I, (I + 2) & 3, at_three(0) + 2 * (I - 1))
            for h in range(2):
                expand(7, 0, h, at_three(0) + (14 - 3 + h))
            dve.wait_ge(x2_ready, NB + 1)
            with dve.Fori(1, NB - 1) as jj:
                J = 7 - jj
                expand_ring(J, 1, 3, at_three(jj))
                for h in range(2):
                    save_acc(h, at_three(jj) + (h - 1), range(2))
                with dve.If(jj < 6):
                    expand_ring(J, 2, 0, at_three(jj) + 2)
                weighed_three(jj - 1)
                own_x2(at_block(jj, CH_2B, C2B, 0), src[:, :])
                turned_three(jj)
                with dve.If(jj < 5):
                    with dve.Fori(3, J + 1) as I:
                        expand_ring(J, I, (I + 2) & 3, at_three(jj) + I * 2 - 2)
                for h in range(2):
                    expand(J, 0, h, at_three(jj + 1) + (h - 5))
            jj = NB - 1
            for h in range(2):
                expand(0, 0, h, at_three(jj) + (h - 1))
            for h in range(2):
                save_acc(h, at_three(jj) + (h - 1), range(2))
            weighed_three(jj - 1)
            own_x2(at_block(jj, CH_2B, C2B, 0), src[:, :])
            turned_three(jj)
            for h in range(2):
                save_acc(h, at_three(jj) + (h + 1), range(2))
            weighed_three(jj)

            with dve.If(unless_binary(dve) > 0):
                dve.wait_ge(product_done, ALL + TWO_A + NB * (NB + 1))
                dve.wait_ge(out_stored, 16 * NB)
                dve.sem_inc(saved_chunk, 1)
                for L in range(3):
                    dve.memset(features[L][:, :, D:D + 1], 1.0).then_inc(steps, 1)

                class General:
                    def __init__(self, base):
                        self.base, self.count = base, 0

                    def step(self, ins):
                        ins.then_inc(steps, 1)
                        self.count += 1
                        dve.wait_ge(steps, self.base + self.count)
                        pass_wait(dve)

                zt, own, square = z[:, 0:D], src[:, 0:D], agg[2][:, 0:D]

                def general_norm(g, powers):
                    g.step(dve.tensor_reduce(mean[:, 0:1], zt, AX.X, ALU.add))
                    g.step(dve.tensor_scalar(mean[:, 0:1], mean[:, 0:1], -1.0 / D, None, ALU.mult))
                    g.step(dve.tensor_scalar(zt, zt, mean[:, 0:1], None, ALU.add))
                    g.step(dve.tensor_tensor(square, zt, zt, ALU.mult))
                    g.step(dve.tensor_reduce(stat[:, 0:1], square, AX.X, ALU.add))
                    g.step(dve.tensor_scalar(stat[:, 0:1], stat[:, 0:1], 1.0 / D, LN_EPS, ALU.mult, ALU.add))
                    dve.wait_ge(rooted, powers)
                    pass_wait(dve)
                    g.step(dve.tensor_scalar(zt, zt, root[:, 0:1], None, ALU.mult))

                for L in range(3):
                    with dve.Fori(0, NT) as J:
                        m = J + L * NT
                        for c in range(CHUNKS):
                            dve.wait_ge(turned_chunk, m * CHUNKS + (c + 3))
                            dve.wait_ge(added_chunk, m * CHUNKS + (c + 1))
                            pass_wait(dve)
                            dve.tensor_copy(agg[0][:, :], acc[0][:, :, :].rearrange("p b n -> p (b n)")
                                            ).then_inc(saved_chunk, 1)
                        g = General(J * GC[L] + g_base[L])
                        dve.wait_ge(added_chunk, m * CHUNKS + (CHUNKS + 1))
                        pass_wait(dve)
                        if L == 2:
                            dve.wait_ge(stored, J * 16 + 16)
                            pass_wait(dve)
                        g.step(dve.tensor_copy(z[:, 0:D + 1], ps_epi[:, 0:D + 1]))
                        g.step(dve.tensor_copy(own, features[L][:, J, 0:D]))
                        dve.wait_ge(small_done, m * 2 + 1)
                        pass_wait(dve)
                        g.step(dve.tensor_copy(featT[:, 0:2 * P], ps_pack[0:D, 0:2 * P]))
                        if L == 0:
                            g.step(dve.tensor_scalar(rdeg[:, 0:1], z[:, D:D + 1], 1.0, 1.0, ALU.add, ALU.max))
                            g.step(dve.reciprocal(rdeg[:, 0:1], rdeg[:, 0:1]))
                            dve.wait_ge(small_done, m * 2 + 2)
                            pass_wait(dve)
                            g.step(dve.tensor_scalar(zt, acc[1][:, 0, 0:D], rdeg[:, 0:1], None, ALU.mult))
                            g.step(dve.tensor_tensor(zt, zt, acc[1][:, 0, 2 * D:3 * D], ALU.add))
                            g.step(dve.tensor_tensor(zt, zt, bias[:, :], ALU.add))
                            g.step(dve.tensor_scalar(zt, zt, 0.0, None, ALU.max))
                            g.step(dve.tensor_tensor(square, zt, zt, ALU.mult))
                            g.step(dve.tensor_reduce(stat[:, 0:1], square, AX.X, ALU.add))
                            g.step(dve.tensor_scalar(stat[:, 0:1], stat[:, 0:1], L2_EPS ** 2, None, ALU.max))
                            dve.wait_ge(rooted, J * 2 + 1)
                            pass_wait(dve)
                            g.step(dve.tensor_scalar(zt, zt, root[:, 0:1], None, ALU.mult))
                            g.step(dve.tensor_tensor(zt, zt, own, ALU.add))
                            general_norm(g, J * 2 + 2)
                            g.step(dve.tensor_copy(features[1][:, J, 0:D], zt))
                        else:
                            dve.wait_ge(small_done, m * 2 + 2)
                            pass_wait(dve)
                            g.step(dve.tensor_copy(zt, acc[1][:, 0, 0:D]))
                            dve.wait_ge(tanned, J + ((L - 1) * NT + 1))
                            pass_wait(dve)
                            if L == 1:
                                g.step(dve.tensor_copy(features[2][:, J, 0:D], zt))
                            else:
                                g.step(dve.tensor_tensor(zt, zt, features[1][:, J, 0:D], ALU.add))
                                general_norm(g, J + (2 * NT + 1))
                        assert g.count == GC[L]


def kernel(x, adj, L0_gnn_W, L0_gnn_b, L1_gnn_W):
    import numpy as np
    import concourse.bacc as bacc
    from concourse.bass_utils import run_bass_kernel_spmd

    nc = bacc.Bacc("TRN2", target_bir_lowering=False, num_devices=1)
    given = {"x": x, "adj": adj, "L0_gnn_W": L0_gnn_W, "L0_gnn_b": L0_gnn_b, "L1_gnn_W": L1_gnn_W}
    arrays = {f"in_{name}": np.ascontiguousarray(a) for name, a in given.items()}
    ins = [nc.dram_tensor(name, a.shape, mybir.dt.from_np(a.dtype), kind="ExternalInput").ap()
           for name, a in arrays.items()]
    out = nc.dram_tensor("out", (N, D), F32, kind="ExternalOutput").ap()
    gnn_kernel(nc, *ins, out)
    return run_bass_kernel_spmd(nc, [arrays], core_ids=[0]).results[0]["out"]
```

```python
from contextlib import ExitStack

import concourse.bass as bass
from concourse import mybir

ALU = mybir.AluOpType
ACT = mybir.ActivationFunctionType
AX = mybir.AxisListType
F32 = mybir.dt.float32
BF16 = mybir.dt.bfloat16
F8 = mybir.dt.float8e4
U8 = mybir.dt.uint8
U32 = mybir.dt.uint32

P = 128
N = 8192
D = 64
BLK = 1024
NB = N // BLK
TB = BLK // P
HALF = BLK // 2
QH = TB // 2
NW = BLK // 16
STEPS = 2 * NB
ALL = STEPS * NB
PAIRS = NB // 2
TWO_A = NB * (NB + 1)

XHI, XMID, XLO, YLO, YHI, YMID, PARTS = 0, 64, 128, 192, 256, 320, 384
GROUPS = 3

ORDER_FIRST = [7, 6, 5, 4, 3, 2, 1, 0]
ORDER_LOW = [7, 6, 5, 4, 3, 0, 1, 2]
ORDER_HIGH = [7, 6, 0, 1, 2, 3, 4, 5]
ORDER_LAST = [7, 0, 1, 2, 3, 4, 5, 6]

LARGE_SLOT = [4] + [(I + 2) % 4 for I in range(1, NB)]
SMALL_SLOT = [5, 1, 2, 0]

USES_1, USES_2 = 6, 4
LN_EPS = 1e-5
L2_EPS = 1e-12


def gnn_kernel(nc, x, adj, w0, b0, w1, out):
    adj_t = adj.rearrange("(j q p) (i c) -> j i p q c", q=TB, p=P, c=BLK)
    x_t = x.rearrange("(j t p) d -> j p t d", t=TB, p=P)
    out_t = out.rearrange("(j t p) d -> j p t d", t=TB, p=P)

    with ExitStack() as ctx:
        def sb(name, shape, dt):
            return ctx.enter_context(nc.sbuf_tensor(name, shape, dt))

        def psum(name, shape, dt):
            return ctx.enter_context(nc.psum_tensor(name, shape, dt))

        def sem(name):
            return ctx.enter_context(nc.semaphore(name))

        packed = sb("packed", [P, NB * NB * 2 * TB * NW], U8)
        raw = sb("raw", [P, 4, 2 * BLK], F32)
        marks = sb("marks", [P, 2, QH, BLK], F8)
        planes = sb("planes", [P, 2, TB, HALF], F8)
        feats = sb("feats", [P, N // P, PARTS], BF16)
        zpart = sb("zpart", [P, NB, TB * D], F32)
        agg = [sb(f"agg{g}", [P, BLK], F32) for g in range(GROUPS)]
        featT = sb("featT", [D, BLK], F32)
        src = sb("src", [P, TB * D], F32)
        z = sb("z", [P, TB * D], F32)
        stage = sb("stage", [P, TB, 2 * P], BF16)
        sq = agg[0][:, 0:TB * D]
        rest = agg[1][:, 0:TB * D]
        nonzero = sb("nonzero", [P, NB * TB, NB], F32)
        ring = raw[:, :, :].rearrange("p u c -> p (u c)").bitcast(F8).rearrange(
            "p (i h a c) -> p i h a c", i=4, h=2, a=TB)
        slot = [ring[:, i] for i in range(4)] + [planes] + [
            marks[:, :, :, :].rearrange("p h q c -> p (h q c)").rearrange("p (h a c) -> p h a c", h=2, a=TB)]
        PLANES, MARKS = 4, 5
        rest_x2 = slot[MARKS].rearrange("p h a c -> p (h a c)")[:, 0:4 * TB * D].bitcast(F32)
        result = [agg[2][:, n * TB * D:(n + 1) * TB * D] for n in range(2)]
        staged_words = stage[:, :, :].rearrange("p t c -> p (t c)").bitcast(F32)
        x1_sum = [staged_words[:, 0:TB * D], z[:, :]]
        sq_out = staged_words[:, TB * D:2 * TB * D]
        packsum = sb("packsum", [P, ALL], F32)
        pow2 = sb("pow2", [P, QH, NW], BF16)
        ident = sb("ident", [P, P], F32)
        bias = sb("bias", [P, D], F32)
        w_self = sb("w_self", [D, 2 * D], F32)
        w_a0 = sb("w_a0", [P, D], F32)
        w_a1 = sb("w_a1", [P, 2 * D], F32)
        w_y = sb("w_y", [P, D], F32)
        w_b1 = sb("w_b1", [P, 2 * D], F32)
        w_x2 = sb("w_x2", [P, D], F32)
        w_y_self = sb("w_y_self", [D, D], F32)
        w_x2_self = sb("w_x2_self", [D, D], F32)
        rdeg = sb("rdeg", [P, TB], F32)
        mean = sb("mean", [P, TB], F32)
        stat = sb("stat", [P, TB], F32)
        root = sb("root", [P, TB], F32)
        minus_half = sb("minus_half", [P, TB], F32)
        ones = sb("ones", [P, 1], F32)
        worth = sb("worth", [P, QH], F32)
        wrong = sb("wrong", [1, 1], F32)
        wrong_int = sb("wrong_int", [1, 1], mybir.dt.int32)

        general = packed[:, :].bitcast(F32)
        each = N // P * (D + 1)
        features = [general[:, n * each:(n + 1) * each].rearrange("p (t d) -> p t d", d=D + 1) for n in range(3)]

        acc = [psum(f"acc{g}", [P, 2, HALF], F32) for g in range(GROUPS)]
        ps_pack = psum("ps_pack", [P, HALF], F32)
        ps_epi = psum("ps_epi", [P, HALF], F32)

        banks = [ps_epi, ps_pack]

        consts = sem("consts")
        bits_ready = sem("bits_ready")
        lo_zeroed = sem("lo_zeroed")
        zeroed = sem("zeroed")
        weights_landed = sem("weights_landed")
        raw_landed = [sem(f"raw_landed{u}") for u in range(4)]
        marked = sem("marked")
        counted = sem("counted")
        pack_done = sem("pack_done")
        pack_saved = sem("pack_saved")
        planes_ready = sem("planes_ready")
        product_done = sem("product_done")
        acc_saved = sem("acc_saved")
        xin_landed = sem("xin_landed")
        xin_landed_2 = sem("xin_landed_2")
        split = sem("split")
        x_ready = sem("x_ready")
        x1_ready = sem("x1_ready")
        x2_ready = sem("x2_ready")
        src_landed = sem("src_landed")
        src_read = sem("src_read")
        epi_filled = sem("epi_filled")
        epi_drained = sem("epi_drained")
        chain = sem("chain")
        half_chain = [sem(f"half_chain{n}") for n in range(2)]
        stat_ready = sem("stat_ready")
        root_ready = sem("root_ready")
        y_ready = sem("y_ready")
        staged = sem("staged")
        summed = sem("summed")
        own_ready = sem("own_ready")
        x1_used = sem("x1_used")
        x1_sum_ready = sem("x1_sum_ready")
        turn_saved = sem("turn_saved")
        weigh_read = sem("weigh_read")
        tanh_done = sem("tanh_done")
        out_ready = sem("out_ready")
        out_stored = [sem(f"out_stored{n}") for n in range(2)]
        sums_ready = sem("sums_ready")
        checked = sem("checked")
        x_landed = sem("x_landed")
        chunk_landed = [sem(f"chunk_landed{n}") for n in range(2)]
        turned_chunk = sem("turned_chunk")
        saved_chunk = sem("saved_chunk")
        added_chunk = sem("added_chunk")
        small_done = sem("small_done")
        steps = sem("steps")
        rooted = sem("rooted")
        tanned = sem("tanned")
        stored = sem("stored")
        passed = sem("passed")

        def pass_wait(eng):
            eng.sem_inc(passed, 1)

        def tiles(ap):
            return ap.rearrange("p (t d) -> p t d", d=D)

        def spread(ap):
            return ap.unsqueeze(2).to_broadcast([P, TB, D])

        def part(J, col):
            return feats[:, bass.ds(J * TB, TB), col:col + D]

        def bytes_of(J, I, h):
            width = TB * NW
            return packed[:, bass.ds(((J * NB + I) * 2 + h) * width, width)]

        def words_of(J, I, h):
            width = TB * NW
            ap = packed[:, bass.ds(((J * NB + I) * 2 + h) * width, width)].bitcast(U32)
            return ap.rearrange("p (a n) -> p a n", a=TB)

        def at_two(jj):
            return jj * (jj + 1) + ALL

        def at_three(m):
            return m * 18 + (ALL + TWO_A)

        C1, C2A, C2B = 17, 2, 8
        EPI_2 = USES_1 * NB
        CH_2A = C1 * (NB - 1) + 7
        CH_2B = CH_2A + C2A * NB

        BITS = 1 + 2 * QH
        CONSTS = 4
        WEIGHTS = 16 * 15

        GC = [22, 5, 12]
        CHECK = 6
        NT = N // P
        CHUNKS = N // BLK
        g_base = [3, 3 + GC[0] * NT, 3 + (GC[0] + GC[1]) * NT]

        def unless_binary(eng):
            eng.wait_ge(checked, CHECK)
            return eng.value_load(wrong_int[:, :], min_val=0, max_val=1 << 24)

        def load_x(eng, first, last, landed):
            eng.dma_start(zpart[:, first:last, :].rearrange("p j (t d) -> p (j t) d", d=D),
                          x[first * BLK:last * BLK, :].rearrange("(n p) d -> p n d", p=P)).then_inc(landed, 16)

        block = ctx.enter_context(nc.Block())

        @block.sync
        def _(sp):
            def load_step(J, I, n, first):
                for u in range(4):
                    if not first:
                        sp.wait_ge(counted, 4 * n + (u - 3))
                        pass_wait(sp)
                    sp.dma_start(raw[:, u, :].rearrange("p (q c) -> p q c", q=2),
                                 adj_t[J, I, :, 2 * u:2 * u + 2, :]).then_inc(raw_landed[u], 16)

            def load_block(J, order, first=False):
                for k, I in enumerate(order):
                    load_step(J, I, J * NB + k, first and k == 0)
                    if k == 5:
                        if not first:
                            sp.wait_ge(src_read, J)
                        sp.dma_start(tiles(src[:, :]), x_t[J]).then_inc(src_landed, 16)

            load_x(sp, NB - 2, NB, xin_landed)
            load_block(0, ORDER_FIRST, first=True)
            load_block(1, ORDER_FIRST)
            with sp.Fori(2, 4) as J:
                load_block(J, ORDER_LOW)
            with sp.Fori(4, NB - 1) as J:
                load_block(J, ORDER_HIGH)
            load_block(NB - 1, ORDER_LAST)
            with sp.Fori(0, PAIRS) as m:
                for n, J in enumerate((7 - m, m)):
                    sp.wait_ge(out_ready, m * 2 + (n + 1))
                    pass_wait(sp)
                    sp.dma_start(out_t[J], tiles(result[n])).then_inc(out_stored[n], 16)
            for n in range(2):
                sp.wait_ge(out_stored[n], 16 * PAIRS)

            with sp.If(unless_binary(sp) > 0):
                sp.wait_ge(product_done, ALL + TWO_A + NB * (NB + 1))
                sp.sem_inc(stored, 16)
                sp.dma_start(features[0][:, :, 0:D], x.rearrange("(t p) d -> p t d", p=P)).then_inc(x_landed, 16)
                for L in range(3):
                    with sp.Fori(0, NT) as J:
                        m = J + L * NT
                        for c in range(CHUNKS):
                            sp.wait_ge(turned_chunk, m * CHUNKS + (c + 1))
                            pass_wait(sp)
                            sp.dma_start(raw[:, c % 2, 0:BLK], adj[bass.ds(J * P, P), c * BLK:(c + 1) * BLK]
                                         ).then_inc(chunk_landed[c % 2], 16)
                        if L == 2:
                            sp.wait_ge(steps, J * GC[2] + (g_base[2] + GC[2]))
                            pass_wait(sp)
                            sp.dma_start(out[bass.ds(J * P, P), :], z[:, 0:D]).then_inc(stored, 16)
                sp.wait_ge(stored, 16 * (NT + 1))

        @block.scalar
        def _(act):
            act.wait_ge(zeroed, 2)
            for dst, src_ap in [
                (w_self[:, 0:D], w0[0:D, :]), (w_self[:, D:2 * D], w0[D:2 * D, :]),
                (w_a0[0:D, :], w0[D:2 * D, :]), (w_a0[D:P, :], w0[D:2 * D, :]),
                (w_a1[0:D, 0:D], w0[D:2 * D, :]), (w_a1[D:P, D:2 * D], w1[0, 0:D, :]),
                (w_y[0:D, :], w1[0, 0:D, :]), (w_y[D:P, :], w1[0, 0:D, :]),
                (w_b1[0:D, D:2 * D], w1[1, 0:D, :]), (w_b1[D:P, 0:D], w1[0, 0:D, :]),
                (w_x2[0:D, :], w1[1, 0:D, :]), (w_x2[D:P, :], w1[1, 0:D, :]),
                (w_y_self[:, :], w1[0, D:2 * D, :]), (w_x2_self[:, :], w1[1, D:2 * D, :]),
                (bias[:, :], b0.rearrange("(a d) -> a d", a=1).to_broadcast([P, D])),
            ]:
                act.dma_start(dst, src_ap).then_inc(weights_landed, 16)

            def count_block(J, order):
                for k, I in enumerate(order):
                    for u in range(4):
                        act.wait_ge(marked, J * 4 * NB + (4 * k + u + 1))
                        for q in range(2):
                            words = raw[:, u, q * BLK:(q + 1) * BLK]
                            ins = act.activation(words, words.bitcast(U32), ACT.Sign,
                                                 accum_out=nonzero[:, bass.ds(J * TB + (2 * u + q), 1), I])
                        ins.then_inc(counted, 1)

            with act.Fori(0, 2) as J:
                count_block(J, ORDER_FIRST)
            with act.Fori(2, 4) as J:
                count_block(J, ORDER_LOW)
            with act.Fori(4, NB - 1) as J:
                count_block(J, ORDER_HIGH)
            count_block(NB - 1, ORDER_LAST)

            def save_turned(b):
                for half in range(2):
                    act.wait_ge(epi_filled, b * USES_2 + (EPI_2 + 1 + half))
                    act.activation(featT[:, half * HALF:(half + 1) * HALF], banks[half][0:D, :],
                                   ACT.Copy).then_inc(turn_saved, 1)

            def save_sums(b, done, groups):
                act.wait_ge(epi_filled, b * USES_2 + EPI_2)
                pass_wait(act)
                for h in range(2):
                    act.wait_ge(product_done, done + (h - 1))
                    for g in groups:
                        ins = act.activation(agg[g][:, h * HALF:(h + 1) * HALF], acc[g][:, h, :], ACT.Copy,
                                             scale=0.5)
                    ins.then_inc(acc_saved, 1)

            def take_tanh(b, ap):
                act.wait_ge(weigh_read, b * 2 + 2)
                act.activation(ap, ap, ACT.Tanh).then_inc(tanh_done, 1)

            act.wait_ge(x1_ready, NB)
            save_turned(0)
            save_sums(0, at_two(1), [1, 2])
            take_tanh(0, z[:, :])
            save_turned(1)
            with act.Fori(2, NB) as b:
                save_sums(b - 1, at_two(b), range(3))
                take_tanh(b - 1, z[:, :])
                save_turned(b)
            save_sums(NB - 1, at_three(0), range(3))
            take_tanh(NB - 1, z[:, :])
            with act.Fori(0, PAIRS) as m:
                b = m * 2 + NB
                save_turned(b)
                save_sums(b, m * 16 + (ALL + TWO_A + STEPS), range(2))
                take_tanh(b, result[0])
                save_turned(b + 1)
                save_sums(b + 1, at_three(m + 1), range(2))
                take_tanh(b + 1, result[1])

            with act.If(unless_binary(act) > 0):
                for L in (1, 2):
                    with act.Fori(0, NT) as J:
                        act.wait_ge(steps, J * GC[L] + (g_base[L] + 4))
                        act.activation(z[:, 0:D], z[:, 0:D], ACT.Tanh).then_inc(tanned, 1)

        @block.gpsimd
        def _(pool):
            load_x(pool, 0, NB - 2, xin_landed_2)
            pool.memset(w_a1[:, :], 0.0).then_inc(zeroed, 1)
            pool.memset(w_b1[:, :], 0.0).then_inc(zeroed, 1)
            pool.memset(pow2[:, :, :], 0.0).then_inc(bits_ready, 1)
            for q in range(QH):
                for half in range(2):
                    pool.wait_ge(bits_ready, 1 + 2 * q + half)
                    pool.affine_select(out=pow2[:, q, :], in_=pow2[:, q, :], compare_op=ALU.not_equal,
                                       fill=float(2 ** (2 * q + half)) / 2, base=-half * NW,
                                       pattern=[[-1, NW]], channel_multiplier=1).then_inc(bits_ready, 1)

            def split_feats(J, ap, col, lo, count, base, done, rest=rest, tiles_of=slice(0, TB)):
                whole, left = tiles(ap)[:, tiles_of], tiles(rest)[:, tiles_of]
                hi, mid, low = (part(J, c)[:, tiles_of] for c in (col, col + D, lo))
                pool.tensor_copy(hi, whole).then_inc(split, 1)
                pool.wait_ge(split, count * 4 + (base + 1))
                pass_wait(pool)
                pool.tensor_tensor(left, whole, hi, ALU.subtract).then_inc(split, 1)
                pool.wait_ge(split, count * 4 + (base + 2))
                pool.tensor_copy(mid, left).then_inc(split, 1)
                pool.wait_ge(split, count * 4 + (base + 3))
                pass_wait(pool)
                pool.tensor_tensor(low, left, mid, ALU.subtract).then_inc(split, 1)
                pool.wait_ge(split, count * 4 + (base + 4))
                pool.sem_inc(done, 1)

            def power(n, cols=slice(0, TB)):
                pool.wait_ge(stat_ready, n)
                pool.tensor_tensor(root[:, cols], stat[:, cols], minus_half[:, cols], ALU.pow).then_inc(root_ready, 1)

            for k, I in enumerate(ORDER_FIRST):
                pool.wait_ge(xin_landed if I >= NB - 2 else xin_landed_2, 16)
                split_feats(I, zpart[:, I, :], XHI, XLO, k, 0, x_ready)
            pool.memset(feats[:, :, YHI:YHI + 2 * D], 0.0).then_inc(consts, 1)
            pool.memset(minus_half[:, :], -0.5).then_inc(consts, 1)
            pool.memset(stage[:, :, 0:D], 0.0).then_inc(x2_ready, 1)
            pool.memset(ident[:, :], 0.0).then_inc(consts, 1)
            pool.wait_ge(consts, 3)
            pool.affine_select(out=ident[:, :], in_=ident[:, :], compare_op=ALU.not_equal, fill=1.0,
                               base=0, pattern=[[-1, P]], channel_multiplier=1).then_inc(consts, 1)

            def epilogue_one(J):
                power(J * 2 + 1)
                power(J * 2 + 2)
                pool.wait_ge(y_ready, J + 1)
                split_feats(J, z[:, :], YHI, YLO, J, 4 * NB, x1_ready)

            with pool.Fori(0, NB - 1) as J:
                epilogue_one(J)
            for n in range(4):
                power(2 * NB - 1 + n, slice(TB // 2 * (n % 2), TB // 2 * (n % 2 + 1)))
            pool.wait_ge(y_ready, NB)
            split_feats(NB - 1, z[:, :], YHI, YLO, NB - 1, 4 * NB, x1_ready, tiles_of=slice(0, TB // 2))
            pool.wait_ge(staged, 1)

            def add_parts(J, into, hi, mid, lo, n, done):
                pool.tensor_tensor(tiles(into), part(J, hi), part(J, mid), ALU.add).then_inc(summed, 1)
                pool.wait_ge(summed, n)
                pass_wait(pool)
                pool.tensor_tensor(tiles(into), tiles(into), part(J, lo), ALU.add).then_inc(done, 1)

            def split_x2(b):
                pool.wait_ge(tanh_done, b + 1)
                pass_wait(pool)
                split_feats(7 - b, z[:, :], XHI, XLO, b, 8 * NB, x2_ready, rest=rest_x2)

            def src_free(b):
                pool.wait_ge(epi_filled, b * USES_2 + (EPI_2 - 2))
                pass_wait(pool)

            add_parts(7, src[:, :], YHI, YMID, YLO, 1, own_ready)
            with pool.Fori(1, NB) as b:
                src_free(b)
                add_parts(7 - b, src[:, :], YHI, YMID, YLO, b + 1, own_ready)
                split_x2(b - 1)
            src_free(NB)
            add_parts(7, src[:, :], XHI, XMID, XLO, NB + 1, own_ready)
            split_x2(NB - 1)

            def sum_x1(m, n):
                add_parts((7 - m, m)[n], x1_sum[n], YHI, YMID, YLO, m * 4 + (NB + 3 + (0, 1)[n]), x1_sum_ready)

            def pair_three(m, last=False):
                src_free(m * 2 + (NB + 1))
                add_parts(m, src[:, :], XHI, XMID, XLO, m * 4 + (NB + 2), own_ready)
                pool.wait_ge(x1_used, m * 2)
                pass_wait(pool)
                sum_x1(m, 0)
                sum_x1(m, 1)
                power(m * 2 + (2 * NB + 3))
                if not last:
                    src_free(m * 2 + (NB + 2))
                    add_parts(6 - m, src[:, :], XHI, XMID, XLO, m * 4 + (NB + 5), own_ready)
                power(m * 2 + (2 * NB + 4))

            with pool.Fori(0, PAIRS - 1) as m:
                pair_three(m)
            pair_three(PAIRS - 1, last=True)

            with pool.If(unless_binary(pool) > 0):
                def general_power(value):
                    pool.wait_ge(steps, value)
                    pool.tensor_tensor(root[:, 0:1], stat[:, 0:1], minus_half[:, 0:1], ALU.pow).then_inc(rooted, 1)

                with pool.Fori(0, NT) as J:
                    general_power(J * GC[0] + (g_base[0] + 12))
                    general_power(J * GC[0] + (g_base[0] + 20))
                with pool.Fori(0, NT) as J:
                    general_power(J * GC[2] + (g_base[2] + 11))

        @block.tensor
        def _(pe):
            def pack(J, s):
                h = s % 2
                pe.wait_ge(marked, J * (2 * STEPS) + (2 * s + 2))
                if not (isinstance(J, int) and s == 0):
                    pe.wait_ge(pack_saved, J * STEPS + s)
                pe.wait_ge(bits_ready, BITS)
                pass_wait(pe)
                for a in range(TB):
                    for q in range(QH):
                        mm = pe.matmul(ps_pack[:, a * NW:(a + 1) * NW], marks[:, h, q, a * P:(a + 1) * P],
                                       pow2[:, q, :], start=q == 0, stop=q == QH - 1)
                mm.then_inc(pack_done, 1)

            def multiply(I, h, groups, start, moving=planes, stationary=None, opens=()):
                pass_wait(pe)
                for a in range(TB):
                    for g in groups:
                        own = feats[:, I * TB + a, g * P:(g + 1) * P] if stationary is None else stationary(a, g)
                        mm = pe.matmul(acc[g][:, h, :], own, moving[:, h, a, :],
                                       start=(start or g in opens) and a == 0, stop=a == TB - 1,
                                       skip_group_check=True)
                return mm

            def turn(half, bank):
                pe.wait_ge(consts, CONSTS)
                pass_wait(pe)
                for t in range(4):
                    tile = 4 * half + t
                    mm = pe.transpose(bank[0:D, t * P:(t + 1) * P], src[:, tile * D:(tile + 1) * D],
                                      ident[:, :])
                mm.then_inc(epi_filled, 1)

            def weigh(bank, first_tile, count, products, width):
                pe.wait_ge(weights_landed, WEIGHTS)
                pass_wait(pe)
                for t in range(count):
                    rows = slice((first_tile + t) * P, (first_tile + t + 1) * P)
                    for n, (lhs, w, col) in enumerate(products):
                        at = t * width + col
                        mm = pe.matmul(bank[:, at:at + w.shape[1]], lhs[:, rows], w, start=n == 0,
                                       stop=n == len(products) - 1, skip_group_check=True)
                mm.then_inc(epi_filled, 1)

            own = featT[:, :]
            ONE = [(own, w_self[:, :], 0), (agg[2], w_y[:, :], 2 * D), (agg[0], w_a0[:, :], D), (agg[1], w_a1[:, :], D)]
            TWO = [(agg[1], w_b1[:, :], 0), (agg[2], w_y[:, :], 0), (own, w_y_self[:, :], 0), (agg[0], w_x2[:, :], D)]
            THREE = [(agg[0], w_x2[:, :], 0), (agg[1][0:D, :], w_x2[0:D, :], 0), (own, w_x2_self[:, :], 0)]

            def epilogue_one(J, piece):
                base = J * USES_1
                if piece == 0:
                    pe.wait_ge(src_landed, J * 16 + 16)
                if piece == 2:
                    pe.wait_ge(acc_saved, J * 2 + 2)
                pe.wait_ge(epi_drained, base + piece)
                if piece < 2:
                    turn(piece, ps_epi)
                else:
                    weigh(ps_epi, 2 * (piece - 2), 2, ONE, 3 * D)

            def block_one(J, order, rows, first=False, last=False):
                slow = order in (ORDER_FIRST, ORDER_LOW)
                opening = order.index(0)
                for s in range(STEPS):
                    k, h = divmod(s, 2)
                    I = order[k]
                    if not (last and s == STEPS - 1):
                        pack(J, s + 1)
                    pe.wait_ge(planes_ready, J * STEPS + (s + 1))
                    if k == 0 and not first:
                        pe.wait_ge(acc_saved, J * 2 + (h - 1))
                    if not first and s == 1 and not slow:
                        epilogue_one(J - 1, 2)
                    if k == 0 and h == 0 and first:
                        pe.wait_ge(lo_zeroed, 1)
                    pe.wait_ge(x_ready, k + 1 if first else NB)
                    least, most = rows
                    if first and k == opening:
                        pe.wait_ge(consts, CONSTS)
                        groups = range(3)
                    elif first or most <= I:
                        groups = range(2)
                    elif I < least:
                        pe.wait_ge(x1_ready, I + 1)
                        groups = range(3)
                    else:
                        with pe.If(J > I):
                            pe.wait_ge(x1_ready, I + 1)
                            multiply(I, h, [2], False)
                        groups = range(2)
                    multiply(I, h, groups, k == 0, opens=[2] if k == opening else []).then_inc(product_done, 1)
                    piece = s + (1 if slow else 2)
                    if not first and s > 0 and piece < 6:
                        epilogue_one(J - 1, piece)
                    if s == STEPS - 1 and not last:
                        epilogue_one(J, 0)
                    if s == STEPS - 2 and last:
                        epilogue_one(J, 0)
                        pe.wait_ge(pack_saved, ALL)
                        turn(1, ps_pack)
                    if not first and s == 0:
                        epilogue_one(J - 1, 1)

            pack(0, 0)
            block_one(0, ORDER_FIRST, (0, 0), first=True)
            block_one(1, ORDER_FIRST, (1, 1))
            with pe.Fori(2, 4) as J:
                block_one(J, ORDER_LOW, (2, 3))
            with pe.Fori(4, NB - 1) as J:
                block_one(J, ORDER_HIGH, (4, 6))
            block_one(NB - 1, ORDER_LAST, (7, 7), last=True)
            pe.wait_ge(epi_drained, USES_1 * NB - 4)
            for pair in range(4):
                pe.wait_ge(acc_saved, 2 * NB - 1 + pair // 2)
                if pair >= 2:
                    pe.wait_ge(epi_drained, USES_1 * NB - 6 + pair + 1)
                weigh(banks[pair % 2], 2 * pair, 2, ONE, 3 * D)
            pe.wait_ge(epi_drained, USES_1 * NB)

            pe.wait_ge(pack_saved, ALL)
            pe.wait_ge(counted, 2 * ALL)
            pe.wait_ge(checked, 3)
            pe.matmul(ps_pack[0:1, 0:ALL], ones[:, :], packsum[:, :], start=True, stop=False)
            counts = nonzero[:, :, :].rearrange("p (j h q) i -> p q j i h", j=NB, h=2)
            for q in range(QH):
                mm = pe.matmul(ps_pack[0:1, 0:ALL], worth[:, q:q + 1], counts[:, q], start=False, stop=q == QH - 1)
            mm.then_inc(sums_ready, 1)

            def turn_block(b):
                pe.wait_ge(own_ready, b + 1)
                for half in range(2):
                    if not isinstance(b, int) or b > 0:
                        pe.wait_ge(weigh_read, b * 2 + (half - 1))
                    turn(half, banks[half])

            def weigh_block(b, products, width):
                pe.wait_ge(acc_saved, b * 2 + (2 * NB + 2))
                pe.wait_ge(turn_saved, b * 2 + 2)
                for half in range(2):
                    weigh(banks[half], 4 * half, 4, products, width)

            def diagonal(jj, h):
                pe.wait_ge(planes_ready, at_two(jj) + (h + 1))
                pe.wait_ge(staged, jj + 1)
                pe.wait_ge(acc_saved, jj * 2 + (2 * NB - 1 + h))
                multiply(None, h, [1, 2], True,
                         stationary=lambda a, g: stage[:, a, (g - 1) * P:g * P]).then_inc(product_done, 1)

            diagonal(0, 0)
            diagonal(0, 1)
            pe.wait_ge(checked, 4)
            turn_block(0)
            with pe.Fori(1, NB) as jj:
                diagonal(jj, 0)
                weigh_block(jj - 1, TWO, 2 * D)
                diagonal(jj, 1)
                for I in range(NB - 1, 0, -1):
                    with pe.If(jj > 7 - I):
                        for h in range(2):
                            pe.wait_ge(planes_ready, at_two(jj) + (2 * (7 - I) + h + 3))
                            pe.wait_ge(x2_ready, 9 - I)
                            multiply(I, h, range(3), False, slot[(7 - I) % 4],
                                     opens=[0] if I == NB - 1 else []).then_inc(product_done, 1)
                    if I == NB - 1:
                        turn_block(jj)

            def lower(done, I, h, where, b=None):
                pe.wait_ge(planes_ready, done + 1)
                if b is not None:
                    pe.wait_ge(acc_saved, b * 2 + (2 * NB - 1 + h))
                pe.wait_ge(x2_ready, NB + 1 if I == 0 else NB)
                multiply(I, h, range(2), b is not None, slot[where]).then_inc(product_done, 1)

            def pair_three(m, first=False):
                b = m * 2 + NB
                at = at_three(m)
                lower(at, 1, 0, LARGE_SLOT[1], b)
                weigh_block(b - 1, *((TWO, 2 * D) if first else (THREE, D)))
                lower(at + 1, 1, 1, LARGE_SLOT[1], b)
                for I in range(2, NB):
                    with ExitStack() as condition:
                        if not first and I > 4:
                            condition.enter_context(pe.If(m < 8 - I))
                        for h in range(2):
                            lower(at + (2 * I - 2 + h), I, h, LARGE_SLOT[I])
                    if I == 3:
                        turn_block(b)
                zero = m * 16 + (ALL + TWO_A + STEPS - 2)
                for h in range(2):
                    lower(zero + h, 0, h, PLANES)
                lower(zero + 2, 0, 0, MARKS, b + 1)
                weigh_block(b, THREE, D)
                lower(zero + 3, 0, 1, MARKS, b + 1)
                if not first:
                    for I in range(1, PAIRS):
                        with pe.If(m > I - 1):
                            for h in range(2):
                                lower(zero + (2 * I + 2 + h), I, h, SMALL_SLOT[I])
                turn_block(b + 1)

            pair_three(0, first=True)
            with pe.Fori(1, PAIRS) as m:
                pair_three(m)
            weigh_block(2 * NB - 1, THREE, D)

            with pe.If(unless_binary(pe) > 0):
                pe.sem_inc(turned_chunk, 2)
                pe.sem_inc(added_chunk, 1)
                pe.wait_ge(x_landed, 16)
                for L in range(3):
                    with pe.Fori(0, NT) as J:
                        m = J + L * NT
                        for c in range(CHUNKS):
                            pe.wait_ge(chunk_landed[c % 2], m * (16 * CHUNKS // 2) + 16 * (c // 2 + 1))
                            pass_wait(pe)
                            if L == 0 and c == 0:
                                pe.wait_ge(steps, 3)
                            pe.wait_ge(saved_chunk, m * CHUNKS + (c + 1))
                            pass_wait(pe)
                            for a in range(TB):
                                mm = pe.transpose(acc[0][:, a // 4, (a % 4) * P:(a % 4 + 1) * P],
                                                  raw[:, c % 2, a * P:(a + 1) * P], ident[:, :])
                            mm.then_inc(turned_chunk, 1)
                            pe.wait_ge(saved_chunk, m * CHUNKS + (c + 2))
                            pass_wait(pe)
                            for a in range(TB):
                                mm = pe.matmul(ps_epi[:, 0:D + 1], agg[0][:, a * P:(a + 1) * P],
                                               features[L][:, c * TB + a, :], start=c + a == 0,
                                               stop=c == CHUNKS - 1 and a == TB - 1)
                            mm.then_inc(added_chunk, 1)
                        at = J * GC[L] + g_base[L]
                        pe.wait_ge(steps, at + 2)
                        pass_wait(pe)
                        pe.transpose(ps_pack[0:D, 0:P], z[:, 0:D], ident[:, :])
                        pe.transpose(ps_pack[0:D, P:2 * P], src[:, 0:D], ident[:, :]).then_inc(small_done, 1)
                        pe.wait_ge(steps, at + 3)
                        pass_wait(pe)
                        if L == 0:
                            pe.matmul(acc[1][:, 0, 0:2 * D], featT[:, P:2 * P], w_self[:, :], start=True, stop=True)
                            pe.matmul(acc[1][:, 0, D:2 * D], featT[:, 0:P], w_a0[0:D, :], start=False, stop=True,
                                      skip_group_check=True).then_inc(small_done, 1)
                        else:
                            w, w_own = (w_y, w_y_self) if L == 1 else (w_x2, w_x2_self)
                            pe.matmul(acc[1][:, 0, 0:D], featT[:, P:2 * P], w_own[:, :], start=True, stop=False)
                            pe.matmul(acc[1][:, 0, 0:D], featT[:, 0:P], w[0:D, :], start=False,
                                      stop=True).then_inc(small_done, 1)

        @block.vector
        def _(dve):
            def mark(J, s, pair, first=False):
                k, h = divmod(s, 2)
                u = 2 * h + pair
                dve.wait_ge(raw_landed[u], J * (16 * NB) + 16 * (k + 1))
                if not first:
                    dve.wait_ge(pack_done, J * STEPS + (s - 1))
                out_ap = marks[:, h, 2 * pair:2 * pair + 2, :].rearrange("p q c -> p (q c)")
                dve.tensor_scalar(out_ap.bitcast(U8), raw[:, u, :], 1.0, 64.0, ALU.is_equal,
                                  ALU.mult).then_inc(marked, 1)

            def save_pack(J, s, I):
                dve.wait_ge(pack_done, J * STEPS + (s + 1))
                dve.tensor_scalar(bytes_of(J, I, s % 2), ps_pack[:, :], 1.0, None, ALU.mult, ALU.add,
                                  accum_out=packsum[:, bass.ds((J * NB + I) * 2 + s % 2, 1)]).then_inc(pack_saved, 1)

            def expand(J, I, h, used, wide=None):
                if used is not None:
                    dve.wait_ge(product_done, used)
                    pass_wait(dve)
                words = words_of(J, I, h)
                wide = planes[:, h, :, :].bitcast(U32) if wide is None else wide
                for bit in range(8):
                    shift, op = (6 - bit, ALU.logical_shift_left) if bit < 7 else (1, ALU.logical_shift_right)
                    ins = dve.tensor_scalar(wide[:, :, bit * NW // 4:(bit + 1) * NW // 4], words, shift,
                                            0x40404040, op, ALU.bitwise_and)
                ins.then_inc(planes_ready, 1)

            def save_acc(h, groups):
                for g in groups:
                    ins = dve.tensor_scalar(agg[g][:, h * HALF:(h + 1) * HALF], acc[g][:, h, :], 0.5, None, ALU.mult)
                if 2 in groups:
                    ins.then_inc(acc_saved, 1)

            class Chain:
                def __init__(self, base, count=0):
                    self.base, self.count = base, count

                def wait(self):
                    dve.wait_ge(chain, self.base + self.count)
                    pass_wait(dve)

                def step(self, ins):
                    ins.then_inc(chain, 1)
                    self.count += 1

            def layernorm(c, z=z[:, :]):
                c.wait()
                c.step(dve.tensor_reduce(mean[:, :], tiles(z), AX.X, ALU.add))
                c.wait()
                c.step(dve.tensor_scalar(mean[:, :], mean[:, :], -1.0 / D, None, ALU.mult))
                c.wait()
                c.step(dve.tensor_tensor(tiles(z), tiles(z), spread(mean[:, :]), ALU.add))

            def variance(c, z=z[:, :], sq=sq):
                c.wait()
                c.step(dve.tensor_tensor(sq, z, z, ALU.mult))
                c.wait()
                c.step(dve.tensor_reduce(stat[:, :], tiles(sq), AX.X, ALU.add))
                c.wait()
                c.step(dve.tensor_scalar(stat[:, :], stat[:, :], 1.0 / D, LN_EPS, ALU.mult, ALU.add))
                c.wait()
                dve.sem_inc(stat_ready, 1)

            def scale(c, root_count, z=z[:, :]):
                dve.wait_ge(root_ready, root_count)
                c.step(dve.tensor_tensor(tiles(z), tiles(z), spread(root[:, :]), ALU.mult))
                c.wait()

            def save_turned(J, half, bank=ps_epi):
                dve.wait_ge(epi_filled, J * USES_1 + (half + 1))
                dve.tensor_copy(featT[:, half * HALF:(half + 1) * HALF], bank[0:D, :]).then_inc(epi_drained, 1)

            def degrees(J):
                c = Chain(J * C1)
                dve.wait_ge(counted, J * (4 * NB) + 4 * NB)
                c.step(dve.tensor_reduce(rdeg[:, :], nonzero[:, bass.ds(J * TB, TB), :], AX.X, ALU.add))
                c.wait()
                c.step(dve.tensor_scalar(rdeg[:, :], rdeg[:, :], 1.0, 1.0, ALU.add, ALU.max))
                c.wait()
                c.step(dve.reciprocal(rdeg[:, :], rdeg[:, :]))
                c.wait()

            def weighed_one(J, pair, bank=ps_epi):
                c = Chain(J * C1, 3 + pair)
                dve.wait_ge(epi_filled, J * USES_1 + (3 + pair))
                cols = slice(2 * pair * D, (2 * pair + 2) * D)
                ps = bank[:, 0:6 * D].rearrange("p (t c) -> p t c", t=2)
                dve.tensor_copy(tiles(zpart[:, J, cols]), ps[:, :, 2 * D:3 * D])
                c.step(dve.tensor_tensor(tiles(z[:, cols]), ps[:, :, D:2 * D],
                                         rdeg[:, 2 * pair:2 * pair + 2].unsqueeze(2).to_broadcast([P, 2, D]),
                                         ALU.mult))
                c.wait()
                dve.tensor_tensor(tiles(z[:, cols]), tiles(z[:, cols]), ps[:, :, 0:D],
                                  ALU.add).then_inc(epi_drained, 1)

            def finish_one(J, n, half=None):
                first, count = (0, TB) if half is None else (half * TB // 2, TB // 2)
                t = slice(first, first + count)
                zt, sqt, xt = tiles(z[:, :])[:, t], tiles(sq)[:, t], tiles(src[:, :])[:, t]

                def wide(ap):
                    return ap[:, t].unsqueeze(2).to_broadcast([P, count, D])

                def step(ins):
                    ins.then_inc(chain if half is None else half_chain[half], 1)

                if n == 0:
                    dve.wait_ge(epi_drained, J * USES_1 + (USES_1 if half != 0 else USES_1 - 2))
                elif n in (4, 12):
                    power = 1 if n == 4 else 2
                    if half is not None:
                        power = 2 * power - 1 + half
                    dve.wait_ge(root_ready, J * 2 + power)
                elif half is None:
                    Chain(J * C1, 7 + n if n < 4 else 6 + n).wait()
                else:
                    dve.wait_ge(half_chain[half], n if n < 4 else n - 1)
                if n == 0:
                    step(dve.tensor_tensor(zt, zt, bias[:, :].unsqueeze(1).to_broadcast([P, count, D]), ALU.add))
                elif n == 1:
                    step(dve.scalar_tensor_tensor(sqt, zt, 0.0, zt, ALU.max, ALU.mult))
                elif n == 2:
                    step(dve.tensor_reduce(stat[:, t], sqt, AX.X, ALU.add))
                elif n == 3:
                    dve.tensor_scalar(stat[:, t], stat[:, t], L2_EPS ** 2, None, ALU.max).then_inc(stat_ready, 1)
                elif n == 4:
                    step(dve.scalar_tensor_tensor(zt, zt, 0.0, wide(root[:, :]), ALU.max, ALU.mult))
                elif n == 5:
                    step(dve.tensor_tensor(zt, zt, xt, ALU.add))
                elif n == 6:
                    if half is None:
                        dve.sem_inc(src_read, 1)
                    step(dve.tensor_reduce(mean[:, t], zt, AX.X, ALU.add))
                elif n == 7:
                    step(dve.tensor_scalar(mean[:, t], mean[:, t], -1.0 / D, None, ALU.mult))
                elif n == 8:
                    step(dve.tensor_tensor(zt, zt, wide(mean[:, :]), ALU.add))
                elif n == 9:
                    step(dve.tensor_tensor(sqt, zt, zt, ALU.mult))
                elif n == 10:
                    step(dve.tensor_reduce(stat[:, t], sqt, AX.X, ALU.add))
                elif n == 11:
                    dve.tensor_scalar(stat[:, t], stat[:, t], 1.0 / D, LN_EPS, ALU.mult,
                                      ALU.add).then_inc(stat_ready, 1)
                else:
                    ins = dve.tensor_tensor(zt, zt, wide(root[:, :]), ALU.mult)
                    ins.then_inc(y_ready if half != 1 else half_chain[1], 1)

            def block_one(J, order, first=False, last=False):
                for s in range(STEPS):
                    nxt = (order + [7])[(s + 1) // 2]
                    more = not (last and s + 1 >= STEPS)
                    over = s + 1 >= STEPS
                    shift = 1 if order in (ORDER_FIRST, ORDER_LOW) else 0
                    late = 3 * (s - shift - 5) + 1

                    def mark_next(pair):
                        if not (last and s + 2 >= STEPS):
                            mark(J, s + 2, pair)

                    mark_next(0)
                    if more:
                        save_pack(J, s + 1, nxt) if not over else save_pack(J + 1, 0, nxt)
                        dve.wait_ge(pack_saved, J * STEPS + (s + 2))
                        expand(J + 1 if over else J, nxt, (s + 1) % 2, None if first and s == 0 else J * STEPS + s)
                    if s == STEPS - 1:
                        dve.wait_ge(x_ready, NB) if first else dve.wait_ge(x1_ready, J)
                        dve.wait_ge(product_done, J * STEPS + (STEPS - 1))
                        pass_wait(dve)
                        save_acc(0, [0, 1])
                    if s == 0 and not first:
                        dve.wait_ge(product_done, J * STEPS)
                        pass_wait(dve)
                        save_acc(1, [0, 1])
                    if s == 1 and not first:
                        degrees(J - 1)
                    if not first and 1 <= s - shift < 5:
                        weighed_one(J - 1, s - shift - 1)
                    if not first and 0 <= late < 13:
                        finish_one(J - 1, late)
                    mark_next(1)
                    if s == STEPS - 1:
                        save_acc(0, [2])
                    if s == 0 and not first:
                        save_acc(1, [2])
                        save_turned(J - 1, 0)
                        save_turned(J - 1, 1)
                    if not first:
                        for n in (late + 1, late + 2):
                            if 0 <= n < 13:
                                finish_one(J - 1, n)

            dve.memset(feats[:, :, YLO:YLO + D], 0.0).then_inc(lo_zeroed, 1)
            for s in range(2):
                for pair in range(2):
                    mark(0, s, pair, first=True)
            save_pack(0, 0, 7)
            dve.wait_ge(pack_saved, 1)
            expand(0, 7, 0, None)
            block_one(0, ORDER_FIRST, first=True)
            dve.memset(ones[:, :], 1.0).then_inc(checked, 1)
            dve.tensor_reduce(worth[:, :], pow2[:, :, :], AX.X, ALU.add).then_inc(checked, 1)
            dve.wait_ge(checked, 2)
            dve.tensor_scalar(worth[:, :], worth[:, :], -2.0, None, ALU.mult).then_inc(checked, 1)
            block_one(1, ORDER_FIRST)
            with dve.Fori(2, 4) as J:
                block_one(J, ORDER_LOW)
            with dve.Fori(4, NB - 1) as J:
                block_one(J, ORDER_HIGH)
            block_one(NB - 1, ORDER_LAST, last=True)
            save_turned(NB - 1, 0)
            save_turned(NB - 1, 1, ps_pack)
            degrees(NB - 1)
            dve.wait_ge(product_done, ALL)
            save_acc(1, range(3))
            for pair in range(2):
                weighed_one(NB - 1, pair, banks[pair])
            for n in range(4):
                finish_one(NB - 1, n, 0)
            weighed_one(NB - 1, 2, banks[0])
            weighed_one(NB - 1, 3, banks[1])
            for n in range(4):
                finish_one(NB - 1, n, 1)
            for n in range(4, 13):
                finish_one(NB - 1, n, 0)
                finish_one(NB - 1, n, 1)
            t = slice(TB // 2, TB)
            whole, left = tiles(z[:, :])[:, t], tiles(sq)[:, t]
            hi, mid, low = (part(NB - 1, c)[:, t] for c in (YHI, YMID, YLO))
            done = 11
            dve.wait_ge(half_chain[1], done)
            dve.tensor_copy(hi, whole).then_inc(half_chain[1], 1)
            dve.wait_ge(half_chain[1], done + 1)
            dve.tensor_tensor(left, whole, hi, ALU.subtract).then_inc(half_chain[1], 1)
            dve.wait_ge(half_chain[1], done + 2)
            dve.tensor_copy(mid, left).then_inc(half_chain[1], 1)
            dve.wait_ge(half_chain[1], done + 3)
            dve.tensor_tensor(low, left, mid, ALU.subtract).then_inc(half_chain[1], 1)
            dve.wait_ge(half_chain[1], done + 4)

            slot32 = [ap.bitcast(U32) for ap in slot]
            ring32 = ring.bitcast(U32)

            def stage_block(jj):
                dve.tensor_copy(stage[:, :, D:2 * P], feats[:, bass.ds((7 - jj) * TB, TB), YLO:PARTS]).then_inc(staged, 1)

            def weighed(b, half):
                dve.wait_ge(epi_filled, b * USES_2 + (EPI_2 + 3 + half))
                pass_wait(dve)
                return slice(4 * half * D, (4 * half + 4) * D)

            def weighed_two(jj):
                J = 7 - jj
                dve.wait_ge(x2_ready, jj + 1)
                for half in range(2):
                    cols = weighed(jj, half)
                    ps = banks[half][:, :].rearrange("p (t c) -> p t c", t=4)
                    dve.tensor_tensor(tiles(z[:, cols]), ps[:, :, 0:D], tiles(zpart[:, J, cols]),
                                      ALU.add).then_inc(chain, 1)
                    dve.wait_ge(chain, jj * C2A + (CH_2A + 1 + half))
                    pass_wait(dve)
                    dve.tensor_copy(tiles(zpart[:, J, cols]), ps[:, :, D:2 * D]).then_inc(weigh_read, 1)

            dve.wait_ge(x1_ready, NB)
            dve.wait_ge(x2_ready, 1)
            dve.wait_ge(counted, 2 * ALL)
            stage_block(0)
            for h in range(2):
                expand(7, 7, h, ALL - 1 + h)
            dve.memset(agg[0][:, :], 0.0)
            dve.wait_ge(sums_ready, 1)
            dve.tensor_reduce(wrong[:, :], ps_pack[0:1, 0:ALL], AX.X, ALU.max,
                              apply_absolute_value=True).then_inc(checked, 1)
            dve.wait_ge(checked, 4)
            dve.tensor_copy(wrong_int[:, :], wrong[:, :]).then_inc(checked, 1)
            dve.wait_ge(checked, 5)
            dve.sem_inc(checked, 1)

            with dve.Fori(1, NB) as jj:
                J = 7 - jj
                dve.wait_ge(product_done, at_two(jj - 1) + 2)
                pass_wait(dve)
                stage_block(jj)
                for h in range(2):
                    expand(J, J, h, None)
                for h in range(2):
                    expand(J, 7, h, at_two(jj) + (h - 1), slot32[0][:, h])
                weighed_two(jj - 1)
                with dve.If(jj > 1):
                    with dve.Fori(1, jj) as m:
                        for h in range(2):
                            expand(J, 7 - m, h, at_two(jj) + m * 2 + (h - 1),
                                   ring32[:, bass.ds(m & 3, 1), h].rearrange("p i a c -> p (i a) c"))

            def expand_three(J, I, n, where):
                for h in range(2):
                    expand(J, I, h, n + (h - 5), slot32[where][:, h])

            def weighed_three(m, n):
                J = (7 - m, m)[n]
                dve.wait_ge(out_stored[n], m * 16)
                pass_wait(dve)
                for half in range(2):
                    cols = weighed(m * 2 + (NB + n), half)
                    dve.tensor_tensor(result[n][:, cols], banks[half][:, 0:4 * D], zpart[:, J, cols],
                                      ALU.add).then_inc(weigh_read, 1)

            def finish_three(m, n):
                b = m * 2 + n
                c = Chain(b * C2B + CH_2B)
                dve.wait_ge(x1_sum_ready, b + 1)
                dve.wait_ge(tanh_done, b + (NB + 1))
                c.step(dve.tensor_tensor(result[n], result[n], x1_sum[n], ALU.add))
                layernorm(c, result[n])
                dve.sem_inc(x1_used, 1)
                variance(c, result[n], sq_out)
                scale(c, b + (2 * NB + 3), result[n])
                dve.sem_inc(out_ready, 1)

            def pair_three(m, first=False):
                at = at_three(m)
                for I in (1, 2):
                    expand_three(7 - m, I, at + (2 * I - 2), LARGE_SLOT[I])
                if first:
                    weighed_two(NB - 1)
                    dve.wait_ge(weigh_read, 2 * NB)
                    dve.wait_ge(x2_ready, NB + 1)
                else:
                    finish_three(m - 1, 0)
                    weighed_three(m - 1, 1)
                for I in range(3, NB):
                    with ExitStack() as condition:
                        if not first and I > 4:
                            condition.enter_context(dve.If(m < 8 - I))
                        expand_three(7 - m, I, at + (2 * I - 2), LARGE_SLOT[I])
                    if I == 4 and not first:
                        finish_three(m - 1, 1)
                zero = m * 16 + (ALL + TWO_A + STEPS - 2)
                expand_three(7 - m, 0, zero, PLANES)
                expand_three(m, 0, zero + 2, MARKS)
                for I in range(1, PAIRS):
                    if not first:
                        with dve.If(m > I - 1):
                            expand_three(m, I, zero + (2 * I + 2), SMALL_SLOT[I])
                    if I == 1:
                        weighed_three(m, 0)

            pair_three(0, first=True)
            with dve.Fori(1, PAIRS) as m:
                pair_three(m)
            finish_three(PAIRS - 1, 0)
            weighed_three(PAIRS - 1, 1)
            finish_three(PAIRS - 1, 1)

            with dve.If(unless_binary(dve) > 0):
                dve.wait_ge(product_done, ALL + TWO_A + NB * (NB + 1))
                for n in range(2):
                    dve.wait_ge(out_stored[n], 16 * PAIRS)
                dve.sem_inc(saved_chunk, 1)
                for L in range(3):
                    dve.memset(features[L][:, :, D:D + 1], 1.0).then_inc(steps, 1)

                class General:
                    def __init__(self, base):
                        self.base, self.count = base, 0

                    def step(self, ins):
                        ins.then_inc(steps, 1)
                        self.count += 1
                        dve.wait_ge(steps, self.base + self.count)
                        pass_wait(dve)

                zt, own, square = z[:, 0:D], src[:, 0:D], agg[2][:, 0:D]

                def general_norm(g, powers):
                    g.step(dve.tensor_reduce(mean[:, 0:1], zt, AX.X, ALU.add))
                    g.step(dve.tensor_scalar(mean[:, 0:1], mean[:, 0:1], -1.0 / D, None, ALU.mult))
                    g.step(dve.tensor_scalar(zt, zt, mean[:, 0:1], None, ALU.add))
                    g.step(dve.tensor_tensor(square, zt, zt, ALU.mult))
                    g.step(dve.tensor_reduce(stat[:, 0:1], square, AX.X, ALU.add))
                    g.step(dve.tensor_scalar(stat[:, 0:1], stat[:, 0:1], 1.0 / D, LN_EPS, ALU.mult, ALU.add))
                    dve.wait_ge(rooted, powers)
                    pass_wait(dve)
                    g.step(dve.tensor_scalar(zt, zt, root[:, 0:1], None, ALU.mult))

                for L in range(3):
                    with dve.Fori(0, NT) as J:
                        m = J + L * NT
                        for c in range(CHUNKS):
                            dve.wait_ge(turned_chunk, m * CHUNKS + (c + 3))
                            dve.wait_ge(added_chunk, m * CHUNKS + (c + 1))
                            pass_wait(dve)
                            dve.tensor_copy(agg[0][:, :], acc[0][:, :, :].rearrange("p b n -> p (b n)")
                                            ).then_inc(saved_chunk, 1)
                        g = General(J * GC[L] + g_base[L])
                        dve.wait_ge(added_chunk, m * CHUNKS + (CHUNKS + 1))
                        pass_wait(dve)
                        if L == 2:
                            dve.wait_ge(stored, J * 16 + 16)
                            pass_wait(dve)
                        g.step(dve.tensor_copy(z[:, 0:D + 1], ps_epi[:, 0:D + 1]))
                        g.step(dve.tensor_copy(own, features[L][:, J, 0:D]))
                        dve.wait_ge(small_done, m * 2 + 1)
                        pass_wait(dve)
                        g.step(dve.tensor_copy(featT[:, 0:2 * P], ps_pack[0:D, 0:2 * P]))
                        if L == 0:
                            g.step(dve.tensor_scalar(rdeg[:, 0:1], z[:, D:D + 1], 1.0, 1.0, ALU.add, ALU.max))
                            g.step(dve.reciprocal(rdeg[:, 0:1], rdeg[:, 0:1]))
                            dve.wait_ge(small_done, m * 2 + 2)
                            pass_wait(dve)
                            g.step(dve.tensor_scalar(zt, acc[1][:, 0, D:2 * D], rdeg[:, 0:1], None, ALU.mult))
                            g.step(dve.tensor_tensor(zt, zt, acc[1][:, 0, 0:D], ALU.add))
                            g.step(dve.tensor_tensor(zt, zt, bias[:, :], ALU.add))
                            g.step(dve.tensor_scalar(zt, zt, 0.0, None, ALU.max))
                            g.step(dve.tensor_tensor(square, zt, zt, ALU.mult))
                            g.step(dve.tensor_reduce(stat[:, 0:1], square, AX.X, ALU.add))
                            g.step(dve.tensor_scalar(stat[:, 0:1], stat[:, 0:1], L2_EPS ** 2, None, ALU.max))
                            dve.wait_ge(rooted, J * 2 + 1)
                            pass_wait(dve)
                            g.step(dve.tensor_scalar(zt, zt, root[:, 0:1], None, ALU.mult))
                            g.step(dve.tensor_tensor(zt, zt, own, ALU.add))
                            general_norm(g, J * 2 + 2)
                            g.step(dve.tensor_copy(features[1][:, J, 0:D], zt))
                        else:
                            dve.wait_ge(small_done, m * 2 + 2)
                            pass_wait(dve)
                            g.step(dve.tensor_copy(zt, acc[1][:, 0, 0:D]))
                            dve.wait_ge(tanned, J + ((L - 1) * NT + 1))
                            pass_wait(dve)
                            if L == 1:
                                g.step(dve.tensor_copy(features[2][:, J, 0:D], zt))
                            else:
                                g.step(dve.tensor_tensor(zt, zt, features[1][:, J, 0:D], ALU.add))
                                general_norm(g, J + (2 * NT + 1))
                        assert g.count == GC[L]


def kernel(x, adj, L0_gnn_W, L0_gnn_b, L1_gnn_W):
    import numpy as np
    import concourse.bacc as bacc
    from concourse.bass_utils import run_bass_kernel_spmd

    nc = bacc.Bacc("TRN2", target_bir_lowering=False, num_devices=1)
    given = {"x": x, "adj": adj, "L0_gnn_W": L0_gnn_W, "L0_gnn_b": L0_gnn_b, "L1_gnn_W": L1_gnn_W}
    arrays = {f"in_{name}": np.ascontiguousarray(a) for name, a in given.items()}
    ins = [nc.dram_tensor(name, a.shape, mybir.dt.from_np(a.dtype), kind="ExternalInput").ap()
           for name, a in arrays.items()]
    out = nc.dram_tensor("out", (N, D), F32, kind="ExternalOutput").ap()
    gnn_kernel(nc, *ins, out)
    return run_bass_kernel_spmd(nc, [arrays], core_ids=[0]).results[0]["out"]
```
